# Optimizing a Trainium2 kernel written in Bass

```python
import numpy as np
import jax
import jax.numpy as jnp

def _softmax(x, axis=-1):
    return jax.nn.softmax(x, axis=axis)

def _gelu(x):
    return jax.nn.gelu(x, approximate=True)

def _silu(x):
    return jax.nn.silu(x)

def _sigmoid(x):
    return jax.nn.sigmoid(x)

def _layernorm(x, axis=-1, eps=1e-05):
    m = jnp.mean(x, axis=axis, keepdims=True)
    v = jnp.var(x, axis=axis, keepdims=True)
    return (x - m) / jnp.sqrt(v + eps)

def _scatter_add(tgt, idx, src, axis=0):
    return tgt.at[idx].add(src)

def _segment_sum(src, seg, n):
    return jax.ops.segment_sum(src, seg, n)
kernel_name = 'mk_vit_tower_d1_tok_img1024_r4_f052ff'

def setup_inputs(seed: int=0):
    np.random.seed(seed)
    _w = jnp.asarray

    def _rec_inputs():
        import jax
        import jax.numpy as jnp
        _rk = jax.random.key(seed)
        x = -0.00016672 + 0.999947 * jax.random.normal(jax.random.fold_in(_rk, 1), (16, 3, 96, 96), jnp.float32)
        return x
    x = _rec_inputs()

    def _L0_tok_setup():
        import jax, jax.numpy as jnp
        import numpy as np
        PATCH = 16
        EPS = 1e-05

        def _patchify(x, p):
            B, C, H, W = x.shape
            hp, wp = (H // p, W // p)
            x = x.reshape(B, C, hp, p, wp, p)
            x = x.transpose(0, 2, 4, 1, 3, 5)
            return x.reshape(B, hp * wp, C * p * p)
        key = jax.random.key(seed)
        ks = jax.random.split(key, 6)
        B, C, H = (64, 3, 96)
        E = 256
        P = PATCH
        N = (H // P) ** 2
        D = C * P * P
        x = jax.random.normal(ks[0], (B, C, H, H), dtype=jnp.float32)
        W = jax.random.normal(ks[1], (D, E), dtype=jnp.float32) * (1.0 / np.sqrt(D))
        b = jnp.zeros((E,), dtype=jnp.float32)
        cls_token = jax.random.normal(ks[2], (1, 1, E), dtype=jnp.float32) * 0.02
        pos_embedding = jax.random.normal(ks[3], (1, N + 1, E), dtype=jnp.float32) * 0.02
        gamma = jnp.ones((E,), dtype=jnp.float32)
        beta = jnp.zeros((E,), dtype=jnp.float32)
        return {'x': x, 'W': W, 'b': b, 'cls_token': cls_token, 'pos_embedding': pos_embedding, 'gamma': gamma, 'beta': beta}
    _L0_tok_all = _L0_tok_setup()
    _L0_tok_in = {k: v for k, v in _L0_tok_all.items() if k in ('W', 'b', 'cls_token', 'pos_embedding', 'gamma', 'beta')}
    del _L0_tok_all

    def _L0_attn_setup():
        import jax, jax.numpy as jnp
        import numpy as np
        E = 256
        H = 16
        HD = E // H
        R = 8
        T, B = (512, 2)

        def _dora_linear(x, m, V, A, Bm, b):
            Vu = V + Bm @ A
            W = m / (jnp.linalg.norm(Vu) + 1e-08) * Vu
            return x @ W.T + b
        key = jax.random.key(seed)
        ks = jax.random.split(key, 16)
        query = jax.random.normal(ks[0], (T, B, E), dtype=jnp.float32)
        kk = jax.random.normal(ks[1], (T, B, E), dtype=jnp.float32)
        vv = jax.random.normal(ks[2], (T, B, E), dtype=jnp.float32)

        def make_dora(k1, k2, k3, k4):
            w = jax.random.normal(k1, (E, E), dtype=jnp.float32) * E ** (-0.5)
            m = jnp.linalg.norm(w)
            V = w / m
            A = jax.random.normal(k2, (R, E), dtype=jnp.float32) * E ** (-0.5)
            Bm = jax.random.normal(k3, (E, R), dtype=jnp.float32) * 0.01
            b = jax.random.normal(k4, (E,), dtype=jnp.float32) * 0.01
            return (m, V, A, Bm, b)
        mag_q, dir_q, A_q, B_q, bias_q = make_dora(ks[3], ks[4], ks[5], ks[6])
        mag_v, dir_v, A_v, B_v, bias_v = make_dora(ks[7], ks[8], ks[9], ks[10])
        k_w = jax.random.normal(ks[11], (E, E), dtype=jnp.float32) * E ** (-0.5)
        k_b = jax.random.normal(ks[12], (E,), dtype=jnp.float32) * 0.01
        out_w = jax.random.normal(ks[13], (E, E), dtype=jnp.float32) * E ** (-0.5)
        out_b = jax.random.normal(ks[14], (E,), dtype=jnp.float32) * 0.01
        return dict(query=query, key=kk, value=vv, mag_q=mag_q, dir_q=dir_q, A_q=A_q, B_q=B_q, bias_q=bias_q, mag_v=mag_v, dir_v=dir_v, A_v=A_v, B_v=B_v, bias_v=bias_v, k_w=k_w, k_b=k_b, out_w=out_w, out_b=out_b)
    _L0_attn_all = _L0_attn_setup()
    _L0_attn_in = {k: v for k, v in _L0_attn_all.items() if k in ('key', 'value', 'mag_q', 'dir_q', 'A_q', 'B_q', 'bias_q', 'mag_v', 'dir_v', 'A_v', 'B_v', 'bias_v', 'k_w', 'k_b', 'out_w', 'out_b')}
    del _L0_attn_all

    def _L0_ffn_setup():
        import jax, jax.numpy as jnp
        import numpy as np
        ALPHA = 1.702
        LIMIT = 7.0
        EPS = 1e-05
        E = 16
        K = 4

        def _swiglu(h):
            x_glu = jnp.minimum(h[..., ::2], LIMIT)
            x_lin = jnp.clip(h[..., 1::2], LIMIT, LIMIT)
            return x_glu * jax.nn.sigmoid(ALPHA * x_glu) * (x_lin + 1.0)
        key = jax.random.key(seed)
        ks = jax.random.split(key, 7)
        B, T, H, I = (1, 512, 256, 256)
        x = jax.random.normal(ks[0], (B, T, H), jnp.float32)
        scale = jnp.ones((H,), jnp.float32)
        gate_w = jax.random.normal(ks[1], (E, H), jnp.float32) * 0.02
        gate_b = jnp.zeros((E,), jnp.float32)
        mlp1_w = jax.random.normal(ks[2], (E, 2 * I, H), jnp.float32) * 0.02
        mlp1_b = jax.random.normal(ks[3], (E, 2 * I), jnp.float32) * 0.02
        mlp2_w = jax.random.normal(ks[4], (E, H, I), jnp.float32) * 0.02
        mlp2_b = jax.random.normal(ks[5], (E, H), jnp.float32) * 0.02
        return dict(x=x, scale=scale, gate_w=gate_w, gate_b=gate_b, mlp1_w=mlp1_w, mlp1_b=mlp1_b, mlp2_w=mlp2_w, mlp2_b=mlp2_b)
    _L0_ffn_all = _L0_ffn_setup()
    _L0_ffn_in = {k: v for k, v in _L0_ffn_all.items() if k in ('scale', 'gate_w', 'gate_b', 'mlp1_w', 'mlp1_b', 'mlp2_w', 'mlp2_b')}
    del _L0_ffn_all
    return {'x': x, 'L0_tok_W': _L0_tok_in['W'], 'L0_tok_b': _L0_tok_in['b'], 'L0_tok_cls_token': _L0_tok_in['cls_token'], 'L0_tok_pos_embedding': _L0_tok_in['pos_embedding'], 'L0_tok_gamma': _L0_tok_in['gamma'], 'L0_tok_beta': _L0_tok_in['beta'], 'L0_attn_key': _L0_attn_in['key'], 'L0_attn_value': _L0_attn_in['value'], 'L0_attn_mag_q': _L0_attn_in['mag_q'], 'L0_attn_dir_q': _L0_attn_in['dir_q'], 'L0_attn_A_q': _L0_attn_in['A_q'], 'L0_attn_B_q': _L0_attn_in['B_q'], 'L0_attn_bias_q': _L0_attn_in['bias_q'], 'L0_attn_mag_v': _L0_attn_in['mag_v'], 'L0_attn_dir_v': _L0_attn_in['dir_v'], 'L0_attn_A_v': _L0_attn_in['A_v'], 'L0_attn_B_v': _L0_attn_in['B_v'], 'L0_attn_bias_v': _L0_attn_in['bias_v'], 'L0_attn_k_w': _L0_attn_in['k_w'], 'L0_attn_k_b': _L0_attn_in['k_b'], 'L0_attn_out_w': _L0_attn_in['out_w'], 'L0_attn_out_b': _L0_attn_in['out_b'], 'L0_ffn_scale': _L0_ffn_in['scale'], 'L0_ffn_gate_w': _L0_ffn_in['gate_w'], 'L0_ffn_gate_b': _L0_ffn_in['gate_b'], 'L0_ffn_mlp1_w': _L0_ffn_in['mlp1_w'], 'L0_ffn_mlp1_b': _L0_ffn_in['mlp1_b'], 'L0_ffn_mlp2_w': _L0_ffn_in['mlp2_w'], 'L0_ffn_mlp2_b': _L0_ffn_in['mlp2_b']}

def reference(x, L0_tok_W, L0_tok_b, L0_tok_cls_token, L0_tok_pos_embedding, L0_tok_gamma, L0_tok_beta, L0_attn_key, L0_attn_value, L0_attn_mag_q, L0_attn_dir_q, L0_attn_A_q, L0_attn_B_q, L0_attn_bias_q, L0_attn_mag_v, L0_attn_dir_v, L0_attn_A_v, L0_attn_B_v, L0_attn_bias_v, L0_attn_k_w, L0_attn_k_b, L0_attn_out_w, L0_attn_out_b, L0_ffn_scale, L0_ffn_gate_w, L0_ffn_gate_b, L0_ffn_mlp1_w, L0_ffn_mlp1_b, L0_ffn_mlp2_w, L0_ffn_mlp2_b):
    import jax
    import jax.numpy as jnp

    def _L0_tok_ref(x, W, b, cls_token, pos_embedding, gamma, beta):
        import jax, jax.numpy as jnp
        import numpy as np
        PATCH = 16
        EPS = 1e-05

        def _patchify(x, p):
            B, C, H, W = x.shape
            hp, wp = (H // p, W // p)
            x = x.reshape(B, C, hp, p, wp, p)
            x = x.transpose(0, 2, 4, 1, 3, 5)
            return x.reshape(B, hp * wp, C * p * p)
        B = x.shape[0]
        patches = _patchify(x, PATCH)
        tok = jnp.einsum('bnd,de->bne', patches, W) + b
        cls = jnp.broadcast_to(cls_token, (B, 1, tok.shape[-1]))
        h = jnp.concatenate([cls, tok], axis=1) + pos_embedding
        mu = jnp.mean(h, axis=-1, keepdims=True)
        var = jnp.mean(jnp.square(h - mu), axis=-1, keepdims=True)
        out = (h - mu) * jax.lax.rsqrt(var + EPS) * gamma + beta
        return out

    def _L0_attn_ref(query, key, value, mag_q, dir_q, A_q, B_q, bias_q, mag_v, dir_v, A_v, B_v, bias_v, k_w, k_b, out_w, out_b):
        import jax, jax.numpy as jnp
        import numpy as np
        E = 256
        H = 16
        HD = E // H
        R = 8
        T, B = (512, 2)

        def _dora_linear(x, m, V, A, Bm, b):
            Vu = V + Bm @ A
            W = m / (jnp.linalg.norm(Vu) + 1e-08) * Vu
            return x @ W.T + b
        Tq, Bq, _ = query.shape
        q = _dora_linear(query, mag_q, dir_q, A_q, B_q, bias_q)
        k = query @ k_w.T + k_b
        v = _dora_linear(query, mag_v, dir_v, A_v, B_v, bias_v)
        q = q.reshape(Tq, Bq * H, HD).transpose(1, 0, 2)
        k = k.reshape(Tq, Bq * H, HD).transpose(1, 0, 2)
        v = v.reshape(Tq, Bq * H, HD).transpose(1, 0, 2)
        scale = HD ** (-0.5)
        attn = jnp.einsum('nqd,nkd->nqk', q, k) * scale
        attn = jax.nn.softmax(attn, axis=-1)
        out = jnp.einsum('nqk,nkd->nqd', attn, v)
        out = out.transpose(1, 0, 2).reshape(Tq, Bq, E)
        out = out @ out_w.T + out_b
        return out

    def _L0_ffn_ref(x, scale, gate_w, gate_b, mlp1_w, mlp1_b, mlp2_w, mlp2_b):
        import jax, jax.numpy as jnp
        import numpy as np
        ALPHA = 1.702
        LIMIT = 7.0
        EPS = 1e-05
        E = 16
        K = 4

        def _swiglu(h):
            x_glu = jnp.minimum(h[..., ::2], LIMIT)
            x_lin = jnp.clip(h[..., 1::2], LIMIT, LIMIT)
            return x_glu * jax.nn.sigmoid(ALPHA * x_glu) * (x_lin + 1.0)
        t = x * jax.lax.rsqrt(jnp.mean(x * x, axis=-1, keepdims=True) + EPS) * scale
        g = jnp.einsum('bth,eh->bte', t, gate_w) + gate_b
        vals, idx = jax.lax.top_k(g, K)
        w = jax.nn.softmax(vals, axis=-1)
        route = jnp.sum(jax.nn.one_hot(idx, E, dtype=t.dtype) * w[..., None], axis=-2)
        route_e = jnp.moveaxis(route, -1, 0)

        def step(acc, p):
            w1, b1, w2, b2, r = p
            h = jnp.einsum('bth,ih->bti', t, w1) + b1
            s = _swiglu(h)
            y = jnp.einsum('bti,hi->bth', s, w2) + b2
            return (acc + r[..., None] * y, None)
        acc, _ = jax.lax.scan(step, jnp.zeros_like(x), (mlp1_w, mlp1_b, mlp2_w, mlp2_b, route_e))
        return x + acc
    h = _L0_tok_ref(x, L0_tok_W, L0_tok_b, L0_tok_cls_token, L0_tok_pos_embedding, L0_tok_gamma, L0_tok_beta)
    h = h + _L0_attn_ref(_layernorm(h, axis=-1), L0_attn_key, L0_attn_value, L0_attn_mag_q, L0_attn_dir_q, L0_attn_A_q, L0_attn_B_q, L0_attn_bias_q, L0_attn_mag_v, L0_attn_dir_v, L0_attn_A_v, L0_attn_B_v, L0_attn_bias_v, L0_attn_k_w, L0_attn_k_b, L0_attn_out_w, L0_attn_out_b)
    h = h + _L0_ffn_ref(_layernorm(h, axis=-1), L0_ffn_scale, L0_ffn_gate_w, L0_ffn_gate_b, L0_ffn_mlp1_w, L0_ffn_mlp1_b, L0_ffn_mlp2_w, L0_ffn_mlp2_b)
    return h

_drawn_inputs = setup_inputs


def setup_inputs(seed=0):
    import zlib

    import numpy as np

    out = dict(_drawn_inputs(seed))
    spreads = {'L0_tok_b': (0.0, 0.1),
     'L0_tok_gamma': (1.0, 0.2),
     'L0_tok_beta': (0.0, 0.1),
     'L0_ffn_scale': (1.0, 0.2),
     'L0_ffn_gate_b': (0.0, 0.1)}
    factors = {'L0_attn_bias_q': 8.0,
     'L0_attn_bias_v': 5.076,
     'L0_attn_k_b': 8.0,
     'L0_attn_out_b': 5.802,
     'L0_ffn_mlp1_b': 8.0,
     'L0_ffn_mlp2_b': 8.0}
    for name, (base, spread) in spreads.items():
        noise = np.random.default_rng([zlib.crc32(name.encode()), seed]).standard_normal(out[name].shape)
        drawn = base * np.exp(spread * noise) if base else spread * noise
        out[name] = jnp.asarray(drawn.astype(out[name].dtype))
    for name, factor in factors.items():
        out[name] = (out[name] * factor).astype(out[name].dtype)
    return out
```

```python
import concourse.bass as bass
from concourse import mybir
from contextlib import ExitStack

P = 128
IMGS, CH, SIDE, PATCH = 16, 3, 96, 16
GRID = SIDE // PATCH
POS = GRID * GRID + 1
TOK = POS * IMGS
D_IN = CH * PATCH * PATCH
E = 256
HEADS, HD = 16, 16
RANK = 8
EXPERTS, TOPK, INNER = 16, 4, 256
KC = E // P
KD = D_IN // P
PPT = P // IMGS
HPC = P // HD
TILES = [(t * P, min(P, TOK - t * P)) for t in range((TOK + P - 1) // P)]
NT = len(TILES)
HALF = TOK // 2
ADD_ROWS = POS + 2
EPS = 1e-5
ALPHA, LIMIT = 1.702, 7.0

W1_AT, W2_AT = 0, KC * 2 * INNER
B1_AT = W2_AT + KC * E
W_COLS = B1_AT + 4
UNITS = 4
RING = 4
LAG = 3


def build(nc, x_t, w_tok, add_rows, add_sel, proj, dora, rows, cols, mags, gate, gate_b, b2, experts, consts, out):
    fp32 = mybir.dt.float32
    ALU = mybir.AluOpType
    ACT = mybir.ActivationFunctionType
    AX = mybir.AxisListType.X

    r_dram = nc.dram_tensor("route_scratch", [EXPERTS, TOK], fp32, kind="Internal").ap()

    with ExitStack() as ctx:
        def sb(name, shape):
            return ctx.enter_context(nc.sbuf_tensor(name, shape, fp32))

        def sem(name):
            return ctx.enter_context(nc.semaphore(name))

        xt = sb("xt", [P, KD, TOK])
        wt = sb("wt", [P, KD, E])
        addr = sb("addr", [ADD_ROWS, E])
        addsel = sb("addsel", [ADD_ROWS, TOK])
        pw = sb("pw", [P, 4, KC, E])
        dr = sb("dr", [RANK, 4, E])
        rowb = sb("rowb", [P, 4, E])
        colb = sb("colb", [P, 3, KC])
        mag = sb("mag", [P, 2])
        gw = sb("gw", [P, KC, EXPERTS])
        gb = sb("gb", [1, EXPERTS])
        b2s = sb("b2s", [EXPERTS, E])
        cst = sb("cst", [P, 2 * P + HPC])
        ident, ones, mask = cst[:, 0:P], cst[:, P:2 * P], cst[:, 2 * P:2 * P + HPC]
        phalf = sb("phalf", [P, 2])

        wqv = sb("wqv", [P, 2, KC, E])
        sq = sb("sq", [P, KC * E])
        ss = sb("ss", [P, 2])
        sst = sb("sst", [P, 2])
        nrm = sb("nrm", [P, 2])
        nrme = sb("nrme", [P, 2])
        nrmi = sb("nrmi", [P, 2])
        dsc = sb("dsc", [P, 2])
        st = sb("st", [P, 3, NT, 6])
        mv = sb("mv", [P, 3, NT, 2])
        ve = sb("ve", [P, 3, NT])
        rs = sb("rs", [P, 3, NT])
        hn = sb("hn", [P, NT, E])
        hg = sb("hg", [P, NT, E])
        h1 = sb("h1", [P, NT, E])
        hb = sb("hb", [P, NT, E])
        x2 = sb("x2", [P, NT, E])
        x2t = sb("x2t", [P, KC, TOK])
        qt = sb("qt", [P, KC, TOK])
        kt = sb("kt", [P, KC, TOK])
        qbd = sb("qbd", [P, KC, POS, HPC, IMGS])
        vs = sb("vs", [P, NT, E])
        mx = sb("mx", [P, NT, KC * PPT])
        sd = sb("sd", [P, NT, E])
        ex = sb("ex", [P, NT, E])
        sm = sb("sm", [P, NT, KC * PPT])
        smi = sb("smi", [P, NT, KC * PPT])
        pr = sb("pr", [P, NT, E])
        ptb = sb("ptb", [P, 2, HEADS, PPT, IMGS])
        os_ = sb("os", [P, NT, E])
        ot = sb("ot", [P, KC, TOK])
        h2 = sb("h2", [P, NT, E])
        ln = hn
        hx = hg
        rq = sb("rq", [P, NT])
        rm = sb("rm", [P, NT])
        re = sb("re", [P, NT])
        rr = sb("rr", [P, NT])
        rsc = sb("rsc", [P, NT])
        tn = sb("tn", [P, NT, E])
        tt = sb("tt", [P, KC, TOK])
        g = sb("g", [P, NT, EXPERTS])
        top = sb("top", [P, NT, 8])
        rep = sb("rep", [P, NT, EXPERTS])
        gmask = sb("gmask", [P, NT, EXPERTS])
        gd = sb("gd", [P, NT, EXPERTS])
        ge = sb("ge", [P, NT, EXPERTS])
        gm = sb("gm", [P, NT, EXPERTS])
        gs = sb("gs", [P, NT])
        gi = sb("gi", [P, NT])
        route = sb("route", [P, NT, EXPERTS])
        rt = sb("rt", [EXPERTS, TOK])
        we = sb("we", [P, 2, W_COLS])
        bl = sb("bl", [P, 2, 2])
        rb = sb("rb", [P, 2, TOK])
        ring = qbd[:, :, :, :, :].rearrange("p c n h q -> p (c n h q)")[:, 0:7 * RING * HALF].rearrange(
            "p (i b n) -> p i b n", i=7, b=RING)
        xg, sg, sr, li, lc, xs, sw = (ring[:, i] for i in range(7))
        res = x2t

        bank = [ctx.enter_context(nc.psum_tensor(f"bank{i}", [P, 512], fp32)) for i in range(8)]

        in_x = [sem(f"in_x{i}") for i in range(2)]
        in_add, in_small, in_proj, in_ffn = sem("in_add"), sem("in_small"), sem("in_proj"), sem("in_ffn")
        w_in = [sem("w_in0"), sem("w_in1")]
        rb_in = [sem("rb_in0"), sem("rb_in1")]
        r_out = sem("r_out")
        y_out = sem("y_out")
        dve_c = sem("dve_chain")
        pool_c = sem("pool_chain")
        half_set = sem("half_set")
        dora_mm, dora_w, dora_sq, dora_sum, dora_tot, dora_nrm, dora_s = (
            sem(n) for n in ("dora_mm", "dora_w", "dora_sq", "dora_sum", "dora_tot", "dora_nrm", "dora_s"))
        emb, var_ready, rstd, hn_done, h1_done = (sem(n) for n in ("emb", "var_ready", "rstd", "hn_done", "h1_done"))
        x2_done, x2t_mm, x2t_done = sem("x2_done"), sem("x2t_mm"), sem("x2t_done")
        qk_mm, qk_done, qbd_done, qbd_pool = sem("qk_mm"), sem("qk_done"), sem("qbd_done"), sem("qbd_pool")
        v_mm, v_done = sem("v_mm"), sem("v_done")
        s_mm, s_sub, s_exp, p_done = sem("s_mm"), sem("s_sub"), sem("s_exp"), sem("p_done")
        pt_mm, pt_act, pt_dve = sem("pt_mm"), sem("pt_act"), sem("pt_dve")
        o_mm, o_done, ot_mm, ot_done = sem("o_mm"), sem("o_done"), sem("ot_mm"), sem("ot_done")
        a_mm, h2_done, hx_done, tn_done, tt_mm, tt_done = sem("a_mm"), sem("h2_done"), sem("hx_done"), sem("tn_done"), sem("tt_mm"), sem("tt_done")
        g_mm, g_sub, g_exp, r_done, rt_mm, rt_done = (
            sem(n) for n in ("g_mm", "g_sub", "g_exp", "r_done", "rt_mm", "rt_done"))
        b1_plus, up_mm, xg_done, li_done, sg_done, sr_done, xs_done, sw_done, down_mm = (
            sem(n) for n in ("b1_plus", "up_mm", "xg_done", "li_done", "sg_done", "sr_done", "xs_done", "sw_done",
                             "down_mm"))
        res_dve, res_act = sem("res_dve"), sem("res_act")

        def acc(c, hf):
            return bank[4 + 2 * c + hf][:, 0:HALF]

        def slot(s):
            w1 = we[:, s, W1_AT:W2_AT].rearrange("p (k m i) -> p k m i", k=KC, m=4)
            w2 = we[:, s, W2_AT:B1_AT].rearrange("p (k m i) -> p k m i", k=KC, m=KC)
            return w1, w2, we[:, s, B1_AT:W_COLS]

        block = ctx.enter_context(nc.Block())

        @block.sync
        def _(sp):
            xsrc = x_t.rearrange("(k p) n -> p k n", p=P)
            wsrc = w_tok.rearrange("(k p) n -> p k n", p=P)
            for i in range(2):
                ks = slice(i * KD // 2, (i + 1) * KD // 2)
                sp.dma_start(wt[:, ks, :], wsrc[:, ks, :]).then_inc(in_x[i], 16)
                sp.dma_start(xt[:, ks, :], xsrc[:, ks, :]).then_inc(in_x[i], 16)
            sp.dma_start(pw[:, :, :, :], proj.rearrange("m (k p) n -> p m k n", p=P)).then_inc(in_proj, 16)

            def load_expert(e, s):
                sp.dma_start(we[:, s, :], experts[bass.ds(e, 1), :, :].rearrange("a p n -> (a p) n")).then_inc(w_in[s], 16)

            def load_route(e, s):
                sp.dma_start(rb[:, s, :], r_dram[bass.ds(e, 1), :].to_broadcast([P, TOK])).then_inc(rb_in[s], 16)

            for s in range(2):
                load_expert(s, s)
            sp.wait_ge(rt_done, NT)
            sp.dma_start(r_dram[:, :], rt[:, :]).then_inc(r_out, 16)
            sp.wait_ge(r_out, 16)
            for s in range(2):
                load_route(s, s)
            with sp.Fori(1, EXPERTS // 2) as i:
                for s in range(2):
                    sp.wait_ge(down_mm, (i - 1) * (2 * UNITS) + UNITS * (s + 1))
                    load_expert(i * 2 + s, s)
                    load_route(i * 2 + s, s)
            for hf in range(2):
                sp.wait_ge(res_dve, hf + 1)
                sp.wait_ge(res_act, hf + 1)
                sp.dma_start(out.rearrange("(k p) n -> p k n", p=P)[:, :, hf * HALF:(hf + 1) * HALF],
                             res[:, :, hf * HALF:(hf + 1) * HALF]).then_inc(y_out, 16)
            sp.wait_ge(y_out, 32)

        @block.gpsimd
        def _(pool):
            n = [0]

            def link(ins):
                n[0] += 1
                ins.then_inc(pool_c, 1)
                pool.wait_ge(pool_c, n[0])

            nc.gpsimd.memset(phalf[:, 0:1], -0.5)
            nc.gpsimd.memset(phalf[:, 1:2], 0.5).then_inc(half_set, 1)
            pool.wait_ge(half_set, 1)
            def inv_root(l, t, rows_):
                nc.gpsimd.tensor_tensor(rs[0:rows_, l, t:t + 1], ve[0:rows_, l, t:t + 1], phalf[0:rows_, 0:1],
                                        ALU.pow).then_inc(rstd, 1)

            for t, (_, n_) in enumerate(TILES):
                pool.wait_ge(var_ready, t + 1)
                inv_root(0, t, n_)
                if t == 0:
                    pool.wait_ge(in_small, 16 * 8)
                pool.wait_ge(hn_done, t + 1)
                link(nc.gpsimd.tensor_tensor(hg[0:n_, t, :], hn[0:n_, t, :], rowb[0:n_, 0, :], ALU.mult))
                nc.gpsimd.tensor_tensor(h1[0:n_, t, :], hg[0:n_, t, :], rowb[0:n_, 1, :], ALU.add).then_inc(h1_done, 1)
            for t, (_, n_) in enumerate(TILES):
                pool.wait_ge(var_ready, NT + t + 1)
                inv_root(1, t, n_)
            pool.wait_ge(dora_tot, 1)
            nc.gpsimd.tensor_tensor(nrm[:, :], sst[:, :], phalf[:, 1:2].to_broadcast([P, 2]), ALU.pow).then_inc(dora_nrm, 1)
            pool.wait_ge(h1_done, NT)
            for t, (_, n_) in enumerate(TILES):
                ins = nc.gpsimd.tensor_tensor(hb[0:n_, t, :], h1[0:n_, t, :], rowb[0:n_, 3, :], ALU.add)
            ins.then_inc(qbd_pool, 1)
            for t, (_, n_) in enumerate(TILES):
                pool.wait_ge(var_ready, 2 * NT + 2 * t + 1)
                inv_root(2, t, n_)
                pool.wait_ge(var_ready, 2 * NT + 2 * t + 2)
                nc.gpsimd.tensor_tensor(rr[0:n_, t:t + 1], re[0:n_, t:t + 1], phalf[0:n_, 0:1], ALU.pow).then_inc(rstd, 1)
            for t, (_, n_) in enumerate(TILES):
                pool.wait_ge(rstd, 2 * NT + 2 * t + 1)
                link(nc.gpsimd.tensor_scalar(ln[0:n_, t, :], h2[0:n_, t, :], mv[0:n_, 2, t, 0:1], rs[0:n_, 2, t:t + 1],
                                             ALU.subtract, ALU.mult))
                nc.gpsimd.tensor_tensor(hx[0:n_, t, :], h2[0:n_, t, :], ln[0:n_, t, :], ALU.add).then_inc(hx_done, 1)

            def unit(at, u):
                b, s, hf = u % RING, u // UNITS, u % 2
                if u % UNITS == 0:
                    pool.wait_ge(rb_in[s], (at + 1) * 16)
                pool.wait_ge(sg_done, at * (2 * UNITS) + u + 1)
                nc.gpsimd.tensor_tensor(sr[:, b, :], sg[:, b, :], rb[:, s, hf * HALF:(hf + 1) * HALF],
                                        ALU.mult).then_inc(sr_done, 1)

            with pool.Fori(0, EXPERTS // 2) as i:
                for u in range(2 * UNITS):
                    unit(i, u)

        @block.scalar
        def _(act):
            for dst, src in ((addr, add_rows), (addsel, add_sel)):
                act.dma_start(dst[:, :], src).then_inc(in_add, 16)
            act.dma_start(cst[:, :], consts).then_inc(in_small, 16)
            act.dma_start(dr[:, :, :], dora).then_inc(in_small, 16)
            act.dma_start(mag[:, :], mags.to_broadcast([P, 2])).then_inc(in_small, 16)
            act.dma_start(rowb[:, :, :], rows.rearrange("(a m) n -> a m n", a=1).to_broadcast([P, 4, E])).then_inc(in_small, 16)
            act.dma_start(colb[:, :, :], cols).then_inc(in_small, 16)
            act.dma_start(gw[:, :, :], gate).then_inc(in_small, 16)
            act.dma_start(gb[:, :], gate_b).then_inc(in_small, 16)
            act.dma_start(b2s[:, :], b2).then_inc(in_small, 16)
            for m in range(2):
                act.wait_ge(dora_w, m + 1)
                if m:
                    act.wait_ge(dora_sq, 1)
                nc.scalar.activation(sq[:, :], wqv[:, m, :, :].rearrange("p k n -> p (k n)"), ACT.Square,
                                     accum_out=ss[:, m:m + 1]).then_inc(dora_sq, 1)
            act.wait_ge(in_small, 16 * 8)
            for t, (at, n_) in enumerate(TILES):
                act.wait_ge(x2t_mm, t + 1)
                nc.scalar.copy(x2t[:, :, at:at + n_], bank[2 + t % 2][:, 0:KC * n_].rearrange("p (k n) -> p k n", k=KC)
                               ).then_inc(x2t_done, 1)
            act.wait_ge(dora_s, 1)
            for hf in range(2):
                for c in range(KC):
                    u = KC * hf + c
                    a, b = hf * HALF, (hf + 1) * HALF
                    act.wait_ge(qk_mm, u + 1)
                    nc.scalar.activation(qt[:, c, a:b], bank[4 + 2 * (u % 2)][:, 0:HALF], ACT.Identity,
                                         bias=colb[:, 0, c:c + 1], scale=dsc[:, 0:1])
                    nc.scalar.activation(kt[:, c, a:b], bank[5 + 2 * (u % 2)][:, 0:HALF], ACT.Identity,
                                         bias=colb[:, 1, c:c + 1]).then_inc(qk_done, 1)
            for t, (at, n_) in enumerate(TILES):
                w = KC * (n_ // IMGS) * IMGS
                act.wait_ge(s_sub, t + 1)
                nc.scalar.activation(ex[:, t, 0:w], sd[:, t, 0:w], ACT.Exp, scale=HD ** -0.5).then_inc(s_exp, 1)
            for t, (at, n_) in enumerate(TILES):
                act.wait_ge(pt_mm, t + 1)
                if t >= 2:
                    act.wait_ge(o_mm, t - 1)
                for j in range(PPT // 2, PPT):
                    if j < n_ // IMGS:
                        ins = nc.scalar.activation(
                            ptb[0:n_, t % 2, :, j, :], bank[t % 2][0:n_, 0:E].rearrange("p (h q) -> p h q", h=HEADS),
                            ACT.Copy, scale=mask[0:n_, j:j + 1])
                ins.then_inc(pt_act, 1)
                if t:
                    act.wait_ge(o_mm, t)
                    m_ = TILES[t - 1][1]
                    nc.scalar.copy(os_[0:m_, t - 1, :], bank[2 + (t - 1) % 2][0:m_, 0:E]).then_inc(o_done, 1)
            act.wait_ge(o_mm, NT)
            m_ = TILES[NT - 1][1]
            nc.scalar.copy(os_[0:m_, NT - 1, :], bank[2 + (NT - 1) % 2][0:m_, 0:E]).then_inc(o_done, 1)
            for t, (at, n_) in enumerate(TILES):
                act.wait_ge(ot_mm, t + 1)
                nc.scalar.copy(ot[:, :, at:at + n_], bank[4 + t % 2][:, 0:KC * n_].rearrange("p (k n) -> p k n", k=KC)
                               ).then_inc(ot_done, 1)
            for t, (at, n_) in enumerate(TILES):
                act.wait_ge(tt_mm, t + 1)
                for c in range(KC):
                    ins = nc.scalar.activation(tt[:, c, at:at + n_], bank[2 + t % 2][:, c * n_:(c + 1) * n_], ACT.Copy,
                                               scale=colb[:, 2, c:c + 1])
                ins.then_inc(tt_done, 1)
            for t, (at, n_) in enumerate(TILES):
                act.wait_ge(g_sub, t + 1)
                nc.scalar.activation(ge[0:n_, t, :], gd[0:n_, t, :], ACT.Exp).then_inc(g_exp, 1)
            for t, (at, n_) in enumerate(TILES):
                act.wait_ge(rt_mm, t + 1)
                nc.scalar.copy(rt[:, at:at + n_], bank[2 + t % 2][0:EXPERTS, 0:n_]).then_inc(rt_done, 1)

            def unit(at, u):
                b, s, j = u % RING, u // UNITS, (u % UNITS) // 2
                if u % UNITS == 0:
                    act.wait_ge(b1_plus, at * 2 + s + 1)
                act.wait_ge(up_mm, at * (2 * UNITS) + u + 1)
                nc.scalar.activation(li[:, b, :], bank[2 * (u % 2) + 1][:, 0:HALF], ACT.Identity,
                                     bias=bl[:, s, j:j + 1]).then_inc(li_done, 1)
                act.wait_ge(xg_done, at * (2 * UNITS) + u + 1)
                nc.scalar.activation(sg[:, b, :], xg[:, b, :], ACT.Sigmoid, scale=ALPHA).then_inc(sg_done, 1)

            with act.Fori(0, EXPERTS // 2) as i:
                for u in range(2 * UNITS):
                    unit(i, u)
            act.wait_ge(down_mm, EXPERTS * UNITS)
            for hf in range(2):
                nc.scalar.copy(res[:, 1, hf * HALF:(hf + 1) * HALF], acc(1, hf)).then_inc(res_act, 1)

        @block.vector
        def _(dve):
            n = [0]

            def link(ins):
                n[0] += 1
                ins.then_inc(dve_c, 1)
                dve.wait_ge(dve_c, n[0])

            dve.wait_ge(in_proj, 16)
            for m in range(2):
                dve.wait_ge(dora_mm, m + 1)
                nc.vector.tensor_tensor(wqv[:, m, :, :], pw[:, m, :, :],
                                        bank[4 + m][:, 0:KC * E].rearrange("p (k n) -> p k n", k=KC),
                                        ALU.add).then_inc(dora_w, 1)

            def stats(ln, t, rows_, src):
                link(nc.vector.bn_stats(st[0:rows_, ln, t, :], src))
                link(nc.vector.bn_aggr(mv[0:rows_, ln, t, :], st[0:rows_, ln, t, :]))
                nc.vector.tensor_scalar_add(ve[0:rows_, ln, t:t + 1], mv[0:rows_, ln, t, 1:2], EPS).then_inc(var_ready, 1)

            def norm(ln, t, rows_, dst, src, done):
                dve.wait_ge(rstd, ln * NT + t + 1)
                nc.vector.tensor_scalar(dst[0:rows_, t, :], src, mv[0:rows_, ln, t, 0:1], rs[0:rows_, ln, t:t + 1],
                                        ALU.subtract, ALU.mult).then_inc(done, 1)

            for t in range(NT + 1):
                if t < NT:
                    dve.wait_ge(emb, t + 1)
                    stats(0, t, TILES[t][1], bank[t % 2][0:TILES[t][1], 0:E])
                if t:
                    norm(0, t - 1, TILES[t - 1][1], hn, bank[(t - 1) % 2][0:TILES[t - 1][1], 0:E], hn_done)
            for t in range(NT + 1):
                if t < NT:
                    dve.wait_ge(h1_done, t + 1)
                    stats(1, t, TILES[t][1], h1[0:TILES[t][1], t, :])
                if t:
                    norm(1, t - 1, TILES[t - 1][1], x2, h1[0:TILES[t - 1][1], t - 1, :], x2_done)
            dve.wait_ge(dora_sum, 1)
            nc.vector.tensor_copy(sst[:, :], bank[6][:, 0:2]).then_inc(dora_tot, 1)
            dve.wait_ge(dora_nrm, 1)
            link(nc.vector.tensor_scalar_add(nrme[:, :], nrm[:, :], 1e-8))
            link(nc.vector.reciprocal(nrmi[:, :], nrme[:, :]))
            nc.vector.tensor_tensor(dsc[:, :], nrmi[:, :], mag[:, :], ALU.mult).then_inc(dora_s, 1)
            dve.wait_ge(dora_s, 1)
            for t, (_, n_) in enumerate(TILES):
                dve.wait_ge(v_mm, t + 1)
                nc.vector.scalar_tensor_tensor(out=vs[0:n_, t, :], in0=bank[t % 2][0:n_, 0:E], scalar=dsc[0:n_, 1:2],
                                               in1=rowb[0:n_, 2, :], op0=ALU.mult, op1=ALU.add).then_inc(v_done, 1)
            dve.wait_ge(qk_done, 2 * KC)
            for c in range(KC):
                for j in range(HPC):
                    ins = nc.vector.tensor_scalar(qbd[:, c, :, j, :], qt[:, c, :].rearrange("p (n q) -> p n q", q=IMGS),
                                                  mask[:, j:j + 1], None, ALU.mult)
            ins.then_inc(qbd_done, 1)
            for t in range(NT + 1):
                if t < NT:
                    gn = KC * (TILES[t][1] // IMGS)
                    sc = bank[4 + t % 2][:, 0:gn * IMGS].rearrange("p (g k) -> p g k", k=IMGS)
                    dve.wait_ge(s_mm, t + 1)
                    link(nc.vector.tensor_reduce(mx[:, t, 0:gn], sc, AX, ALU.max))
                    nc.vector.tensor_tensor(sd[:, t, 0:gn * IMGS].rearrange("p (g k) -> p g k", k=IMGS), sc,
                                            mx[:, t, 0:gn].unsqueeze(2).to_broadcast([P, gn, IMGS]),
                                            ALU.subtract).then_inc(s_sub, 1)
                if t:
                    gn = KC * (TILES[t - 1][1] // IMGS)
                    e3 = ex[:, t - 1, 0:gn * IMGS].rearrange("p (g k) -> p g k", k=IMGS)
                    dve.wait_ge(s_exp, t)
                    link(nc.vector.tensor_reduce(sm[:, t - 1, 0:gn], e3, AX, ALU.add))
                    link(nc.vector.reciprocal(smi[:, t - 1, 0:gn], sm[:, t - 1, 0:gn]))
                    nc.vector.tensor_tensor(pr[:, t - 1, 0:gn * IMGS].rearrange("p (g k) -> p g k", k=IMGS), e3,
                                            smi[:, t - 1, 0:gn].unsqueeze(2).to_broadcast([P, gn, IMGS]),
                                            ALU.mult).then_inc(p_done, 1)
            for t, (_, n_) in enumerate(TILES):
                dve.wait_ge(pt_act, t + 1)
                if t >= 2:
                    dve.wait_ge(o_mm, t - 1)
                for j in range(PPT // 2):
                    if j < n_ // IMGS:
                        ins = nc.vector.tensor_scalar(
                            ptb[0:n_, t % 2, :, j, :], bank[t % 2][0:n_, 0:E].rearrange("p (h q) -> p h q", h=HEADS),
                            mask[0:n_, j:j + 1], None, ALU.mult)
                ins.then_inc(pt_dve, 1)
            dve.wait_ge(qbd_pool, 1)
            for t, (_, n_) in enumerate(TILES):
                dve.wait_ge(a_mm, t + 1)
                nc.vector.tensor_tensor(h2[0:n_, t, :], bank[t % 2][0:n_, 0:E], hb[0:n_, t, :], ALU.add).then_inc(h2_done, 1)
                dve.wait_ge(h2_done, t + 1)
                stats(2, t, n_, h2[0:n_, t, :])
                raise_ = 2 * NT + 2 * t
                dve.wait_ge(rstd, raise_ + 1)
                one = slice(t, t + 1)
                link(nc.vector.tensor_tensor(rq[0:n_, one], rs[0:n_, 2, one], rs[0:n_, 2, one], ALU.mult))
                link(nc.vector.tensor_tensor(rm[0:n_, one], rq[0:n_, one], mv[0:n_, 2, t, 1:2], ALU.mult))
                nc.vector.tensor_scalar_add(re[0:n_, one], rm[0:n_, one], EPS).then_inc(var_ready, 1)
                dve.wait_ge(rstd, raise_ + 2)
                link(nc.vector.tensor_tensor(rsc[0:n_, one], rs[0:n_, 2, one], rr[0:n_, one], ALU.mult))
                nc.vector.tensor_scalar(tn[0:n_, t, :], h2[0:n_, t, :], mv[0:n_, 2, t, 0:1], rsc[0:n_, one],
                                        ALU.subtract, ALU.mult).then_inc(tn_done, 1)
            for t, (_, n_) in enumerate(TILES):
                dve.wait_ge(g_mm, t + 1)
                link(nc.vector.tensor_copy(g[0:n_, t, :], bank[t % 2][0:n_, 0:EXPERTS]))
                link(nc.vector.max(top[0:n_, t, :], g[0:n_, t, :]))
                nc.vector.tensor_scalar(gd[0:n_, t, :], g[0:n_, t, :], top[0:n_, t, 0:1], None,
                                        ALU.subtract).then_inc(g_sub, 1)
                link(nc.vector.memset(top[0:n_, t, TOPK:8], -3.0e38))
                link(nc.vector.match_replace(rep[0:n_, t, :], top[0:n_, t, :], g[0:n_, t, :], 3.0e38))
                link(nc.vector.tensor_single_scalar(gmask[0:n_, t, :], rep[0:n_, t, :], 2.9e38, ALU.is_ge))
                dve.wait_ge(g_exp, t + 1)
                link(nc.vector.tensor_tensor(gm[0:n_, t, :], ge[0:n_, t, :], gmask[0:n_, t, :], ALU.mult))
                link(nc.vector.tensor_reduce(gs[0:n_, t:t + 1], gm[0:n_, t, :], AX, ALU.add))
                link(nc.vector.reciprocal(gi[0:n_, t:t + 1], gs[0:n_, t:t + 1]))
                nc.vector.tensor_scalar(route[0:n_, t, :], gm[0:n_, t, :], gi[0:n_, t:t + 1], None,
                                        ALU.mult).then_inc(r_done, 1)

            def first(at, u):
                b, s, j = u % RING, u // UNITS, (u % UNITS) // 2
                _, _, b1 = slot(s)
                if u % UNITS == 0:
                    dve.wait_ge(w_in[s], (at + 1) * 16)
                    nc.vector.tensor_scalar_add(bl[:, s, :], b1[:, 2:4], 1.0).then_inc(b1_plus, 1)
                dve.wait_ge(up_mm, at * (2 * UNITS) + u + 1)
                nc.vector.tensor_scalar(xg[:, b, :], bank[2 * (u % 2)][:, 0:HALF], b1[:, j:j + 1], LIMIT,
                                        ALU.add, ALU.min).then_inc(xg_done, 1)

            def second(at, u):
                b = u % RING
                dve.wait_ge(sr_done, at * (2 * UNITS) + u + 1)
                nc.vector.tensor_scalar(lc[:, b, :], li[:, b, :], LIMIT + 1, LIMIT + 1, ALU.max, ALU.min)
                nc.vector.tensor_tensor(xs[:, b, :], xg[:, b, :], sr[:, b, :], ALU.mult).then_inc(xs_done, 1)
                dve.wait_ge(xs_done, at * (2 * UNITS) + u + 1)
                if isinstance(at, int):
                    if u >= RING:
                        dve.wait_ge(down_mm, at * (2 * UNITS) + u + 1 - RING)
                else:
                    dve.wait_ge(down_mm, at * (2 * UNITS) + u + 1 - RING)
                nc.vector.tensor_tensor(sw[:, b, :], xs[:, b, :], lc[:, b, :], ALU.mult).then_inc(sw_done, 1)

            for u in range(2 * UNITS):
                first(0, u)
                if u:
                    second(0, u - 1)
            with dve.Fori(1, EXPERTS // 2) as i:
                for u in range(2 * UNITS):
                    first(i, u)
                    second(i - 1 if u == 0 else i, (u - 1) % (2 * UNITS))
            second(EXPERTS // 2 - 1, 2 * UNITS - 1)
            dve.wait_ge(down_mm, EXPERTS * UNITS)
            for hf in range(2):
                nc.vector.tensor_copy(res[:, 0, hf * HALF:(hf + 1) * HALF], acc(0, hf)).then_inc(res_dve, 1)

        @block.tensor
        def _(pe):
            mm = nc.tensor.matmul
            pe.wait_ge(in_small, 16 * 8)
            for m in range(2):
                for k in range(KC):
                    ins = mm(bank[4 + m][:, k * E:(k + 1) * E], dr[:, 2 * m, k * P:(k + 1) * P], dr[:, 2 * m + 1, :],
                             start=(k == 0), stop=True, skip_group_check=True)
                ins.then_inc(dora_mm, 1)
            pe.wait_ge(in_add, 32)
            for t, (at, n_) in enumerate(TILES):
                if t >= 2:
                    pe.wait_ge(hn_done, t - 1)
                o = bank[t % 2][0:n_, 0:E]
                mm(o, addsel[:, at:at + n_], addr[:, :], start=True, stop=False)
                for k in range(KD):
                    if t == 0 and k % (KD // 2) == 0:
                        pe.wait_ge(in_x[k // (KD // 2)], 32)
                    ins = mm(o, xt[:, k, at:at + n_], wt[:, k, :], start=False, stop=(k == KD - 1))
                ins.then_inc(emb, 1)
            pe.wait_ge(dora_sq, 2)
            mm(bank[6][:, 0:2], ones, ss[:, :], start=True, stop=True).then_inc(dora_sum, 1)

            def turn(dst, src, n_, done):
                for c in range(KC):
                    ins = nc.tensor.transpose(dst[:, c * n_:(c + 1) * n_], src[:, c * P:(c + 1) * P], ident[0:n_, 0:n_])
                ins.then_inc(done, 1)

            for t, (at, n_) in enumerate(TILES):
                pe.wait_ge(x2_done, t + 1)
                if t >= 2:
                    pe.wait_ge(x2t_done, t - 1)
                turn(bank[2 + t % 2], x2[0:n_, t, :], n_, x2t_mm)
            pe.wait_ge(x2t_done, NT)
            pe.wait_ge(dora_tot, 1)
            for hf in range(2):
                for c in range(KC):
                    u = KC * hf + c
                    if u >= 2:
                        pe.wait_ge(qk_done, u - 1)
                    for w, o in ((wqv[:, 0], bank[4 + 2 * (u % 2)]), (pw[:, 2], bank[5 + 2 * (u % 2)])):
                        for k in range(KC):
                            ins = mm(o[:, 0:HALF], w[:, k, c * P:(c + 1) * P], x2t[:, k, hf * HALF:(hf + 1) * HALF],
                                     start=(k == 0), stop=(k == KC - 1))
                    ins.then_inc(qk_mm, 1)
            for t, (at, n_) in enumerate(TILES):
                if t >= 2:
                    pe.wait_ge(v_done, t - 1)
                for k in range(KC):
                    ins = mm(bank[t % 2][0:n_, 0:E], x2t[:, k, at:at + n_], wqv[:, 1, k, :], start=(k == 0),
                             stop=(k == KC - 1))
                ins.then_inc(v_mm, 1)
            pe.wait_ge(qbd_done, 1)
            for t, (at, n_) in enumerate(TILES):
                if t >= 2:
                    pe.wait_ge(s_sub, t - 1)
                pn = n_ // IMGS
                for c in range(KC):
                    for j in range(pn):
                        pos = t * PPT + j
                        o = (c * pn + j) * IMGS
                        ins = mm(bank[4 + t % 2][:, o:o + IMGS], qbd[:, c, pos, :, :].rearrange("p h q -> p (h q)"),
                                 kt[:, c, pos * IMGS:(pos + 1) * IMGS], start=True, stop=True)
                ins.then_inc(s_mm, 1)

            def turn_p(t):
                n_ = TILES[t][1]
                pe.wait_ge(p_done, t + 1)
                if t >= 2:
                    pe.wait_ge(pt_dve, t - 1)
                for c in range(KC):
                    ins = nc.tensor.transpose(bank[t % 2][0:n_, c * P:(c + 1) * P], pr[:, t, c * n_:(c + 1) * n_], ident)
                ins.then_inc(pt_mm, 1)

            pe.wait_ge(v_done, NT)
            turn_p(0)
            for t, (at, n_) in enumerate(TILES):
                if t + 1 < NT:
                    turn_p(t + 1)
                pe.wait_ge(pt_act, t + 1)
                pe.wait_ge(pt_dve, t + 1)
                if t >= 2:
                    pe.wait_ge(o_done, t - 1)
                for h in range(HEADS):
                    ins = mm(bank[2 + t % 2][0:n_, h * HD:(h + 1) * HD],
                             ptb[0:n_, t % 2, h, 0:n_ // IMGS, :].rearrange("p n q -> p (n q)"),
                             vs[0:n_, t, h * HD:(h + 1) * HD], start=True, stop=True)
                ins.then_inc(o_mm, 1)
            for t, (at, n_) in enumerate(TILES):
                pe.wait_ge(o_done, t + 1)
                if t >= 2:
                    pe.wait_ge(ot_done, t - 1)
                turn(bank[4 + t % 2], os_[0:n_, t, :], n_, ot_mm)
            for t, (at, n_) in enumerate(TILES):
                pe.wait_ge(ot_done, t + 1)
                if t >= 2:
                    pe.wait_ge(h2_done, t - 1)
                for k in range(KC):
                    ins = mm(bank[t % 2][0:n_, 0:E], ot[:, k, at:at + n_], pw[:, 3, k, :], start=(k == 0),
                             stop=(k == KC - 1))
                ins.then_inc(a_mm, 1)
            for t, (at, n_) in enumerate(TILES):
                pe.wait_ge(tn_done, t + 1)
                if t >= 2:
                    pe.wait_ge(tt_done, t - 1)
                turn(bank[2 + t % 2], tn[0:n_, t, :], n_, tt_mm)
            pe.wait_ge(tt_done, NT)
            for t, (at, n_) in enumerate(TILES):
                if t >= 2:
                    pe.wait_ge(r_done, t - 1)
                o = bank[t % 2][0:n_, 0:EXPERTS]
                for k in range(KC):
                    mm(o, tt[:, k, at:at + n_], gw[:, k, :], start=(k == 0), stop=False)
                mm(o, ones[0:1, 0:n_], gb[:, :], start=False, stop=True).then_inc(g_mm, 1)
            for t, (at, n_) in enumerate(TILES):
                pe.wait_ge(r_done, t + 1)
                if t >= 2:
                    pe.wait_ge(rt_done, t - 1)
                nc.tensor.transpose(bank[2 + t % 2][0:EXPERTS, 0:n_], route[0:n_, t, :], ident[0:n_, 0:n_]
                                    ).then_inc(rt_mm, 1)
            pe.wait_ge(rt_done, NT)
            pe.wait_ge(hx_done, NT)
            for c in range(KC):
                for hf in range(2):
                    lo, hi = hf * HALF, (hf + 1) * HALF
                    mm(acc(c, hf), b2s[:, c * P:(c + 1) * P], rt[:, lo:hi], start=True, stop=False)
                    for t, (at, n_) in enumerate(TILES):
                        a, b = max(at, lo), min(at + n_, hi)
                        if a < b:
                            mm(acc(c, hf)[:, a - lo:b - lo], hx[0:n_, t, c * P:(c + 1) * P], ident[0:n_, a - at:b - at],
                               start=False, stop=False)

            def up(at, u):
                s, j, hf = u // UNITS, (u % UNITS) // 2, u % 2
                w1, _, _ = slot(s)
                if u % UNITS == 0:
                    pe.wait_ge(w_in[s], (at + 1) * 16)
                if not isinstance(at, int) or at * 2 * UNITS + u >= 2:
                    pe.wait_ge(xg_done, at * (2 * UNITS) + u - 1)
                    pe.wait_ge(li_done, at * (2 * UNITS) + u - 1)
                for m in range(2):
                    for k in range(KC):
                        ins = mm(bank[2 * (u % 2) + m][:, 0:HALF], w1[:, k, 2 * m + j, :],
                                 tt[:, k, hf * HALF:(hf + 1) * HALF], start=(k == 0), stop=(k == KC - 1))
                ins.then_inc(up_mm, 1)

            def down(at, u, last=False):
                s, j, hf, b = u // UNITS, (u % UNITS) // 2, u % 2, u % RING
                _, w2, _ = slot(s)
                pe.wait_ge(sw_done, at * (2 * UNITS) + u + 1)
                for c in range(KC):
                    ins = mm(acc(c, hf), w2[:, j, c, :], sw[:, b, :], start=False, stop=last)
                ins.then_inc(down_mm, 1)

            for u in range(LAG):
                up(0, u)
            with pe.Fori(0, EXPERTS // 2 - 1) as i:
                for u in range(2 * UNITS):
                    down(i, u)
                    if u + LAG < 2 * UNITS:
                        up(i, u + LAG)
                    else:
                        up(i + 1, u + LAG - 2 * UNITS)
            for u in range(2 * UNITS):
                down(EXPERTS // 2 - 1, u, u >= 2 * UNITS - 2)
                if u + LAG < 2 * UNITS:
                    up(EXPERTS // 2 - 1, u + LAG)


def kernel(**inputs):
    import numpy as np
    import concourse.bacc as bacc
    from concourse import mybir as mb
    from concourse.bass_utils import run_bass_kernel_spmd as run

    a = {k: np.asarray(v) for k, v in inputs.items()}
    f = np.float32
    x = a["x"].reshape(IMGS, CH, GRID, PATCH, GRID, PATCH).transpose(1, 3, 5, 2, 4, 0).reshape(D_IN, TOK - IMGS)
    x_t = np.concatenate([np.zeros((D_IN, IMGS), f), x], axis=1)
    add_rows = np.concatenate([a["L0_tok_pos_embedding"][0], a["L0_tok_b"][None], a["L0_tok_cls_token"][0]])
    sel = np.zeros((ADD_ROWS, TOK), f)
    for p in range(POS):
        sel[p, p * IMGS:(p + 1) * IMGS] = 1
    sel[POS, IMGS:] = 1
    sel[POS + 1, :IMGS] = 1

    def col(v):
        return v.reshape(KC, P).T

    w1 = a["L0_ffn_mlp1_w"].reshape(EXPERTS, INNER, 2, KC, P).transpose(0, 4, 3, 2, 1).reshape(EXPERTS, P, -1)
    w2 = a["L0_ffn_mlp2_w"].reshape(EXPERTS, E, KC, P).transpose(0, 3, 2, 1).reshape(EXPERTS, P, -1)
    b1 = a["L0_ffn_mlp1_b"].reshape(EXPERTS, KC, P, 2).transpose(0, 2, 3, 1).reshape(EXPERTS, P, 4)
    consts = np.zeros((P, 2 * P + HPC), f)
    consts[:, :P] = np.eye(P)
    consts[:, P:2 * P] = 1
    consts[np.arange(P), 2 * P + np.arange(P) // HD] = 1
    arrays = {
        "x_t": x_t, "w_tok": a["L0_tok_W"], "add_rows": add_rows, "add_sel": sel,
        "proj": np.stack([a["L0_attn_dir_q"].T, a["L0_attn_dir_v"].T, a["L0_attn_k_w"].T, a["L0_attn_out_w"].T]),
        "dora": np.stack([a["L0_attn_A_q"], a["L0_attn_B_q"].T, a["L0_attn_A_v"], a["L0_attn_B_v"].T], axis=1),
        "rows": np.stack([a["L0_tok_gamma"], a["L0_tok_beta"], a["L0_attn_bias_v"], a["L0_attn_out_b"]]),
        "cols": np.stack([col(a["L0_attn_bias_q"]), col(a["L0_attn_k_b"]), col(a["L0_ffn_scale"])], axis=1),
        "mags": np.stack([a["L0_attn_mag_q"], a["L0_attn_mag_v"]]).reshape(1, 2),
        "gate": a["L0_ffn_gate_w"].T.reshape(KC, P, EXPERTS).transpose(1, 0, 2),
        "gate_b": a["L0_ffn_gate_b"].reshape(1, EXPERTS), "b2": a["L0_ffn_mlp2_b"],
        "experts": np.concatenate([w1, w2, b1], axis=2), "consts": consts,
    }
    arrays = {k: np.ascontiguousarray(v) for k, v in arrays.items()}
    nc = bacc.Bacc("TRN2", target_bir_lowering=False, num_devices=1)
    args = [nc.dram_tensor(f"in_{k}", v.shape, mb.dt.from_np(v.dtype), kind="ExternalInput").ap()
            for k, v in arrays.items()]
    out = nc.dram_tensor("out", [E, TOK], mb.dt.float32, kind="ExternalOutput").ap()
    build(nc, *args, out)
    r = run(nc, [{f"in_{k}": v for k, v in arrays.items()}], core_ids=[0])
    return r.results[0]["out"].reshape(E, POS, IMGS).transpose(2, 1, 0).copy()
```

```python
import concourse.bass as bass
from concourse import mybir
from contextlib import ExitStack

P = 128
IMGS, CH, SIDE, PATCH = 16, 3, 96, 16
GRID = SIDE // PATCH
POS = GRID * GRID + 1
TOK = POS * IMGS
D_IN = CH * PATCH * PATCH
E = 256
HEADS, HD = 16, 16
RANK = 8
EXPERTS, TOPK, INNER = 16, 4, 256
KC = E // P
KD = D_IN // P
PPT = P // IMGS
HPC = P // HD
TILES = [(t * P, min(P, TOK - t * P)) for t in range((TOK + P - 1) // P)]
NT = len(TILES)
HALF = TOK // 2
ADD_ROWS = POS + 2
EPS = 1e-5
ALPHA, LIMIT = 1.702, 7.0

W1_AT, W2_AT = 0, KC * 2 * INNER
B1_AT = W2_AT + KC * E
PIECES = [0, 352, 704, W2_AT, B1_AT]
W_COLS = B1_AT + 4
UNITS = 4
PADW = P - HD
FRESH, ATTN, ROUTE = 0, 1, 2
RING = 4
LAG = 4


def build(nc, x_t, w_tok, add_rows, add_sel, proj, dora, rows, cols, mags, gate, gate_b, b2, experts, consts, out):
    fp32, fp32r = mybir.dt.float32, mybir.dt.float32r
    ALU = mybir.AluOpType
    ACT = mybir.ActivationFunctionType
    AX = mybir.AxisListType.X

    r_dram = nc.dram_tensor("route_scratch", [EXPERTS, TOK], fp32, kind="Internal").ap()

    with ExitStack() as ctx:
        def sb(name, shape, dt=fp32):
            return ctx.enter_context(nc.sbuf_tensor(name, shape, dt))

        def sem(name):
            return ctx.enter_context(nc.semaphore(name))

        xt = sb("xt", [P, KD * TOK])
        wt = sb("wt", [P, KD, E])
        addr = sb("addr", [ADD_ROWS, E])
        addsel = sb("addsel", [ADD_ROWS, TOK])
        pw = sb("pw", [P, 4, KC, E])
        dr = sb("dr", [RANK, 4, E])
        rowb = sb("rowb", [P, 4, E])
        colb = sb("colb", [P, 3, KC])
        mag = sb("mag", [P, 2])
        gw = sb("gw", [P, KC, EXPERTS])
        gb = sb("gb", [1, EXPERTS])
        b2s = sb("b2s", [EXPERTS, E])
        cst = sb("cst", [P, 2 * P + HPC])
        ident, ones, mask = cst[:, 0:P], cst[:, P:2 * P], cst[:, 2 * P:2 * P + HPC]
        phalf = sb("phalf", [P, 2])

        wqv = sb("wqv", [P, 2, KC, E])
        sq = sb("sq", [P, KC * E])
        ss = sb("ss", [P, 2])
        sst = sb("sst", [P, 2])
        nrm = sb("nrm", [P, 2])
        nrme = sb("nrme", [P, 2])
        nrmi = sb("nrmi", [P, 2])
        dsc = sb("dsc", [P, 2])
        st = sb("st", [P, 3, NT, 6])
        mv = sb("mv", [P, 3, NT, 2])
        ve = sb("ve", [P, 3, NT, 2])
        rs = sb("rs", [P, 3, NT, 2])
        ln = sb("ln", [P, 2, E])
        hg = sb("hg", [P, 2, E])
        h1 = sb("h1", [P, 2, E])
        hb = sb("hb", [P, 2, E])
        x2 = sb("x2", [P, 2, E])
        x2t = sb("x2t", [P, 2, KC, P])
        qt = sb("qt", [P, 2, KC, P])
        kt = sb("kt", [P, KC, PADW + TOK])
        qbd = sb("qbd", [P, KC, POS, HPC, IMGS])
        vs = sb("vs", [P, 2, PADW + E])
        mx = sb("mx", [P, NT, KC * PPT])
        sd = sb("sd", [P, 2, E])
        ex = sb("ex", [P, 2, E])
        sm = sb("sm", [P, NT, KC * PPT])
        smi = sb("smi", [P, NT, KC * PPT])
        pr = sb("pr", [P, 2, E])
        ptb = sb("ptb", [P, HEADS, PPT, IMGS])
        os_ = sb("os", [P, 2, E])
        ot = sb("ot", [P, 2, KC, P])
        h2 = sb("h2", [P, 2, E])
        hx = sb("hx", [P, NT, E])
        tn = sb("tn", [P, 2, E])
        tt = sb("tt", [P, KC, TOK])
        g = sb("g", [P, NT, EXPERTS])
        top = sb("top", [P, NT, 8])
        rep = sb("rep", [P, NT, EXPERTS])
        gmask = sb("gmask", [P, NT, EXPERTS])
        gd = sb("gd", [P, NT, EXPERTS])
        ge = sb("ge", [P, NT, EXPERTS])
        gm = sb("gm", [P, NT, EXPERTS])
        gs = sb("gs", [P, NT])
        gi = sb("gi", [P, NT])
        route = sb("route", [P, NT, EXPERTS])
        rt = sb("rt", [EXPERTS, TOK])
        we = sb("we", [P, 2, W_COLS])
        whi = sb("whi", [P, 2, B1_AT], fp32r)
        wlo = sb("wlo", [P, 2, B1_AT], fp32r)
        thi = sb("thi", [P, KC, TOK], fp32r)
        tlo = sb("tlo", [P, KC, TOK], fp32r)
        shi = sb("shi", [P, RING, HALF], fp32r)
        slo = sb("slo", [P, RING, HALF], fp32r)
        bb = sb("bb", [P, 2, 4])
        rb = sb("rb", [P, 2, TOK])
        ring = qbd[:, :, :, :, :].rearrange("p c n h q -> p (c n h q)")

        def ring_of(at, n):
            return ring[:, at * HALF:(at + n) * HALF].rearrange("p (b n) -> p b n", b=n)

        xg, sg, sr, li, sw = (ring_of(i * RING, RING) for i in range(5))
        lc, xs = ring_of(5 * RING, 2), ring_of(5 * RING + 2, 2)
        res = xt[:, 0:KC * TOK].rearrange("p (k n) -> p k n", k=KC)

        bank = [ctx.enter_context(nc.psum_tensor(f"bank{i}", [P, 512], fp32)) for i in range(8)]

        in_w = sem("in_w")
        in_x = [sem(f"in_x{t}") for t in range(NT)]
        in_add, in_dora, in_small, in_gate = sem("in_add"), sem("in_dora"), sem("in_small"), sem("in_gate")
        in_qv, in_ko = sem("in_qv"), sem("in_ko")
        w_in = [sem("w_in0"), sem("w_in1")]
        rb_in = [sem("rb_in0"), sem("rb_in1")]
        r_out = sem("r_out")
        y_out = sem("y_out")
        dve_c = sem("dve_chain")
        pool_c = sem("pool_chain")
        set_up = sem("set_up")
        dora_mm, dora_w, dora_sq, dora_sum, dora_tot, dora_nrm, dora_s = (
            sem(n) for n in ("dora_mm", "dora_w", "dora_sq", "dora_sum", "dora_tot", "dora_nrm", "dora_s"))
        emb, hg_done, h1_done, hb_done = sem("emb"), sem("hg_done"), sem("h1_done"), sem("hb_done")
        var = [sem(f"var{i}") for i in range(3)]
        rstd = [sem(f"rstd{i}") for i in range(3)]
        x2_done, x2t_mm, x2t_done = sem("x2_done"), sem("x2t_mm"), sem("x2t_done")
        qk_mm, q_done, qk_done, qbd_dve, qbd_pool = (
            sem(n) for n in ("qk_mm", "q_done", "qk_done", "qbd_dve", "qbd_pool"))
        v_mm, v_done = sem("v_mm"), sem("v_done")
        s_mm, s_sub, s_exp, p_done = sem("s_mm"), sem("s_sub"), sem("s_exp"), sem("p_done")
        pt_mm, pt_act, pt_dve = sem("pt_mm"), sem("pt_act"), sem("pt_dve")
        o_mm, o_done, ot_mm, ot_done = sem("o_mm"), sem("o_done"), sem("ot_mm"), sem("ot_done")
        a_mm, h2_done, hx_done, tn_done, tt_mm, tt_done = (
            sem(n) for n in ("a_mm", "h2_done", "hx_done", "tn_done", "tt_mm", "tt_done"))
        g_mm, g_read, g_sub, gm_done, g_exp, r_done, rt_mm, rt_done = (
            sem(n) for n in ("g_mm", "g_read", "g_sub", "gm_done", "g_exp", "r_done", "rt_mm", "rt_done"))
        w_hi, w_lo, bb_done, thi_done, tlo_done = (sem(n) for n in ("w_hi", "w_lo", "bb_done", "thi_done", "tlo_done"))
        up_mm, xg_done, li_done, sg_done, sr_done, xs_done, sw_done, hi_done, lo_done, down_mm = (
            sem(n) for n in ("up_mm", "xg_done", "li_done", "sg_done", "sr_done", "xs_done", "sw_done", "hi_done",
                             "lo_done", "down_mm"))
        res_dve, res_act = sem("res_dve"), sem("res_act")

        def acc(c, hf):
            return bank[4 + 2 * c + hf][:, 0:HALF]

        def in_flight(step):
            return [step - lag if 0 <= step - lag < NT else None for lag in (FRESH, ATTN, ROUTE)]

        def groups(t):
            pn = TILES[t][1] // IMGS
            return [(c, j, min(4, pn - j)) for c in range(KC) for j in range(0, pn, 4)]

        group_at = [sum(len(groups(i)) for i in range(t)) for t in range(NT + 1)]
        V_GROUPS = HEADS // 4
        E_BANK, T_BANK, Q_BANK, P_BANK = bank[4:8]

        def w1(w, s):
            return w[:, s, W1_AT:W2_AT].rearrange("p (k m i) -> p k m i", k=KC, m=4)

        def w2(w, s):
            return w[:, s, W2_AT:B1_AT].rearrange("p (k m i) -> p k m i", k=KC, m=KC)

        def next_in(eng, at, s):
            eng.wait_ge(w_in[1 - s], 16 * (at + 1 + s))

        block = ctx.enter_context(nc.Block())

        @block.sync
        def _(sp):
            sp.dma_start(wt[:, :, :], w_tok.rearrange("(k p) n -> p k n", p=P)).then_inc(in_w, 16)
            psrc = proj.rearrange("m (k p) n -> p m k n", p=P)
            for t, (at, n_) in enumerate(TILES):
                sp.dma_start(xt[:, KD * at:KD * (at + n_)], x_t[:, KD * at:KD * (at + n_)]).then_inc(in_x[t], 16)
                if t == 0:
                    for m in range(2):
                        sp.dma_start(pw[:, m], psrc[:, m]).then_inc(in_qv, 16)
                    for m in range(2, 4):
                        sp.dma_start(pw[:, m], psrc[:, m]).then_inc(in_ko, 16)

            def load_expert(e, s):
                sp.dma_start(we[:, s, :], experts[bass.ds(e, 1), :, :].rearrange("a p n -> (a p) n")).then_inc(w_in[s], 16)

            def load_route(e, s):
                sp.dma_start(rb[:, s, :], r_dram[bass.ds(e, 1), :].to_broadcast([P, TOK])).then_inc(rb_in[s], 16)

            for s in range(2):
                load_expert(s, s)
            sp.wait_ge(rt_done, NT)
            sp.dma_start(r_dram[:, :], rt[:, :]).then_inc(r_out, 16)
            sp.wait_ge(r_out, 16)
            for s in range(2):
                load_route(s, s)
            with sp.Fori(1, EXPERTS // 2) as i:
                for s in range(2):
                    sp.wait_ge(w_lo, i * (2 * UNITS) + UNITS * (s - 1))
                    sp.wait_ge(bb_done, i * 2 + s - 1)
                    load_expert(i * 2 + s, s)
                    sp.wait_ge(sr_done, i * (2 * UNITS) + UNITS * (s - 1))
                    load_route(i * 2 + s, s)
            for hf in range(2):
                sp.wait_ge(res_dve, hf + 1)
                sp.wait_ge(res_act, hf + 1)
                sp.dma_start(out.rearrange("(k p) n -> p k n", p=P)[:, :, hf * HALF:(hf + 1) * HALF],
                             res[:, :, hf * HALF:(hf + 1) * HALF]).then_inc(y_out, 16)
            sp.wait_ge(y_out, 32)

        @block.gpsimd
        def _(pool):
            n = [0]

            def link(ins):
                n[0] += 1
                ins.then_inc(pool_c, 1)
                pool.wait_ge(pool_c, n[0])

            for dst, value in ((phalf[:, 0:1], -0.5), (phalf[:, 1:2], 0.5), (kt[:, :, 0:PADW], 0.0), (vs[:, :, 0:PADW], 0.0)):
                nc.gpsimd.memset(dst, value).then_inc(set_up, 1)
            pool.wait_ge(set_up, 4)

            def inv_root(l, t, w):
                n_ = TILES[t][1]
                pool.wait_ge(var[l], t + 1)
                nc.gpsimd.tensor_tensor(rs[0:n_, l, t, 0:w], ve[0:n_, l, t, 0:w], phalf[0:n_, 0:1].to_broadcast([n_, w]),
                                        ALU.pow).then_inc(rstd[l], 1)

            for step in range(NT + ROUTE):
                fresh, _, route_t = in_flight(step)
                if route_t is not None:
                    inv_root(2, route_t, 2)
                if fresh is not None:
                    inv_root(0, fresh, 1)
                    inv_root(1, fresh, 1)
                if step == 0:
                    pool.wait_ge(dora_tot, 1)
                    nc.gpsimd.tensor_tensor(nrm[:, :], sst[:, :], phalf[:, 1:2].to_broadcast([P, 2]),
                                            ALU.pow).then_inc(dora_nrm, 1)
                if route_t is not None:
                    t, n_ = route_t, TILES[route_t][1]
                    pool.wait_ge(rstd[2], t + 1)
                    link(nc.gpsimd.tensor_scalar(ln[0:n_, t % 2, :], h2[0:n_, t % 2, :], mv[0:n_, 2, t, 0:1], rs[0:n_, 2, t, 0:1],
                                                 ALU.subtract, ALU.mult))
                    nc.gpsimd.tensor_tensor(hx[0:n_, t, :], h2[0:n_, t % 2, :], ln[0:n_, t % 2, :], ALU.add).then_inc(hx_done, 1)
                    at = TILES[t][0]
                    pool.wait_ge(thi_done, t + 1)
                    nc.gpsimd.tensor_tensor(tlo[:, :, at:at + n_], tt[:, :, at:at + n_], thi[:, :, at:at + n_],
                                            ALU.subtract).then_inc(tlo_done, 1)
                if fresh is not None:
                    t, (at, n_) = fresh, TILES[fresh]
                    pool.wait_ge(h1_done, t + 1)
                    nc.gpsimd.tensor_tensor(hb[0:n_, t % 2, :], h1[0:n_, t % 2, :], rowb[0:n_, 3, :], ALU.add).then_inc(hb_done, 1)
                    pool.wait_ge(q_done, t + 1)
                    pn, pos = n_ // IMGS, at // IMGS
                    nc.gpsimd.tensor_tensor(
                        qbd[:, 1, pos:pos + pn, :, :],
                        qt[:, t % 2, 1, 0:n_].rearrange("p (n q) -> p n q", q=IMGS).unsqueeze(2).to_broadcast([P, pn, HPC, IMGS]),
                        mask.unsqueeze(1).unsqueeze(3).to_broadcast([P, pn, HPC, IMGS]), ALU.mult).then_inc(qbd_pool, 1)

            def split_lo(s, j, n):
                pool.wait_ge(w_hi, n)
                a, b = PIECES[j], PIECES[j + 1]
                nc.gpsimd.tensor_tensor(wlo[:, s, a:b], we[:, s, a:b], whi[:, s, a:b], ALU.subtract).then_inc(w_lo, 1)

            def unit(at, u, split):
                b, s, hf = u % RING, u // UNITS, u % 2
                if u % UNITS == 0:
                    pool.wait_ge(rb_in[s], (at + 1) * 16)
                pool.wait_ge(sg_done, at * (2 * UNITS) + u + 1)
                nc.gpsimd.tensor_tensor(sr[:, b, :], sg[:, b, :], rb[:, s, hf * HALF:(hf + 1) * HALF],
                                        ALU.mult).then_inc(sr_done, 1)
                if split:
                    split_lo(1 - s, u % UNITS, at * (2 * UNITS) + u + UNITS + 1)

            for j in range(UNITS):
                split_lo(0, j, j + 1)
            with pool.Fori(0, EXPERTS // 2 - 1) as i:
                for u in range(2 * UNITS):
                    unit(i, u, True)
            for u in range(2 * UNITS):
                unit(EXPERTS // 2 - 1, u, u < UNITS)

        @block.scalar
        def _(act):
            act.dma_start(dr[:, :, :], dora).then_inc(in_dora, 16)
            for dst, src in ((addr, add_rows), (addsel, add_sel)):
                act.dma_start(dst[:, :], src).then_inc(in_add, 16)
            act.dma_start(rowb[:, :, :], rows.rearrange("(a m) n -> a m n", a=1).to_broadcast([P, 4, E])).then_inc(in_small, 16)
            act.dma_start(cst[:, :], consts).then_inc(in_small, 16)
            act.dma_start(colb[:, :, :], cols).then_inc(in_small, 16)
            act.dma_start(mag[:, :], mags.to_broadcast([P, 2])).then_inc(in_small, 16)
            act.dma_start(gw[:, :, :], gate).then_inc(in_gate, 16)
            act.dma_start(gb[:, :], gate_b).then_inc(in_gate, 16)
            act.dma_start(b2s[:, :], b2).then_inc(in_gate, 16)
            for m in range(2):
                act.wait_ge(dora_w, m + 1)
                if m:
                    act.wait_ge(dora_sq, 1)
                nc.scalar.activation(sq[:, :], wqv[:, m, :, :].rearrange("p k n -> p (k n)"), ACT.Square,
                                     accum_out=ss[:, m:m + 1]).then_inc(dora_sq, 1)
            act.wait_ge(in_small, 16 * 4)
            for step in range(NT + ROUTE):
                fresh, attn, route_t = in_flight(step)
                if route_t is not None:
                    at, n_ = TILES[route_t]
                    act.wait_ge(tt_mm, route_t + 1)
                    for c in range(KC):
                        ins = nc.scalar.activation(tt[:, c, at:at + n_], Q_BANK[:, c * n_:(c + 1) * n_], ACT.Copy,
                                                   scale=colb[:, 2, c:c + 1])
                    ins.then_inc(tt_done, 1)
                    for c in range(KC):
                        ins = nc.scalar.activation(thi[:, c, at:at + n_], Q_BANK[:, c * n_:(c + 1) * n_], ACT.Copy,
                                                   scale=colb[:, 2, c:c + 1])
                    ins.then_inc(thi_done, 1)
                if fresh is not None:
                    at, n_ = TILES[fresh]
                    act.wait_ge(x2t_mm, fresh + 1)
                    nc.scalar.copy(x2t[:, fresh % 2, :, 0:n_], T_BANK[:, 0:KC * n_].rearrange("p (k n) -> p k n", k=KC)
                                   ).then_inc(x2t_done, 1)
                if attn is not None:
                    w = KC * TILES[attn][1]
                    act.wait_ge(s_sub, group_at[attn + 1])
                    nc.scalar.activation(ex[:, attn % 2, 0:w], sd[:, attn % 2, 0:w], ACT.Exp, scale=HD ** -0.5).then_inc(s_exp, 1)
                if route_t is not None:
                    n_ = TILES[route_t][1]
                    act.wait_ge(g_sub, route_t + 1)
                    nc.scalar.activation(ge[0:n_, route_t, :], gd[0:n_, route_t, :], ACT.Exp).then_inc(g_exp, 1)
                if fresh is not None:
                    at, n_ = TILES[fresh]
                    act.wait_ge(dora_s, 1)
                    act.wait_ge(qk_mm, fresh + 1)
                    for c in range(KC):
                        ins = nc.scalar.activation(qt[:, fresh % 2, c, 0:n_], Q_BANK[:, c * P:c * P + n_], ACT.Identity,
                                                   bias=colb[:, 0, c:c + 1], scale=dsc[:, 0:1])
                    ins.then_inc(q_done, 1)
                    for c in range(KC):
                        ins = nc.scalar.activation(kt[:, c, PADW + at:PADW + at + n_],
                                                   Q_BANK[:, (KC + c) * P:(KC + c) * P + n_], ACT.Identity,
                                                   bias=colb[:, 1, c:c + 1])
                    ins.then_inc(qk_done, 1)
                if attn is not None:
                    n_ = TILES[attn][1]
                    act.wait_ge(pt_mm, attn + 1)
                    if attn:
                        act.wait_ge(o_mm, V_GROUPS * attn)
                    for j in range(PPT // 2):
                        ins = nc.scalar.activation(ptb[0:n_, :, j, :], P_BANK[0:n_, 0:E].rearrange("p (h q) -> p h q", h=HEADS),
                                                   ACT.Copy, scale=mask[0:n_, j:j + 1])
                    ins.then_inc(pt_act, 1)
                if route_t is not None:
                    at, n_ = TILES[route_t]
                    act.wait_ge(rt_mm, route_t + 1)
                    nc.scalar.copy(rt[:, at:at + n_], T_BANK[0:EXPERTS, 0:n_]).then_inc(rt_done, 1)
                if attn is not None:
                    at, n_ = TILES[attn]
                    for gi_ in range(V_GROUPS):
                        k = V_GROUPS * attn + gi_
                        act.wait_ge(o_mm, k + 1)
                        nc.scalar.copy(os_[0:n_, attn % 2, gi_ * 4 * HD:(gi_ + 1) * 4 * HD].rearrange("p (h d) -> p h d", h=4),
                                       bank[2 + k % 2][0:n_, :].rearrange("p (h w) -> p h w", h=4)[:, :, PADW:P]
                                       ).then_inc(o_done, 1)
                    act.wait_ge(ot_mm, attn + 1)
                    nc.scalar.copy(ot[:, attn % 2, :, 0:n_], T_BANK[:, 0:KC * n_].rearrange("p (k n) -> p k n", k=KC)
                                   ).then_inc(ot_done, 1)

            def split_hi(s, j):
                a, b = PIECES[j], PIECES[j + 1]
                nc.scalar.copy(whi[:, s, a:b], we[:, s, a:b]).then_inc(w_hi, 1)

            def round_s(at, u):
                act.wait_ge(sw_done, at * (2 * UNITS) + u + 1)
                nc.scalar.copy(shi[:, u % RING, :], sw[:, u % RING, :]).then_inc(hi_done, 1)

            def unit(at, u, split):
                b, s, j = u % RING, u // UNITS, (u % UNITS) // 2
                if u % UNITS == 0:
                    act.wait_ge(bb_done, at * 2 + s + 1)
                act.wait_ge(up_mm, at * (2 * UNITS) + u + 1)
                nc.scalar.activation(li[:, b, :], bank[2 * (u % 2) + 1][:, 0:HALF], ACT.Identity,
                                     bias=bb[:, s, 2 + j:3 + j]).then_inc(li_done, 1)
                act.wait_ge(xg_done, at * (2 * UNITS) + u + 1)
                nc.scalar.activation(sg[:, b, :], xg[:, b, :], ACT.Sigmoid, scale=ALPHA).then_inc(sg_done, 1)
                if split:
                    if u % UNITS == 0:
                        next_in(act, at, s)
                    split_hi(1 - s, u % UNITS)

            act.wait_ge(w_in[0], 16)
            for j in range(UNITS):
                split_hi(0, j)
            for u in range(2 * UNITS):
                unit(0, u, True)
                if u:
                    round_s(0, u - 1)
            with act.Fori(1, EXPERTS // 2 - 1) as i:
                for u in range(2 * UNITS):
                    unit(i, u, True)
                    round_s(i - 1 if u == 0 else i, (u - 1) % (2 * UNITS))
            for u in range(2 * UNITS):
                unit(EXPERTS // 2 - 1, u, u < UNITS)
                round_s(EXPERTS // 2 - (2 if u == 0 else 1), (u - 1) % (2 * UNITS))
            round_s(EXPERTS // 2 - 1, 2 * UNITS - 1)
            act.wait_ge(down_mm, EXPERTS * UNITS)
            for hf in range(2):
                nc.scalar.copy(res[:, 1, hf * HALF:(hf + 1) * HALF], acc(1, hf)).then_inc(res_act, 1)

        @block.vector
        def _(dve):
            n = [0]

            def link(ins):
                n[0] += 1
                ins.then_inc(dve_c, 1)
                dve.wait_ge(dve_c, n[0])

            def spread(dst, src, m):
                return nc.vector.tensor_scalar(dst, src, m, None, ALU.mult)

            def stats(l, t, src):
                n_ = TILES[t][1]
                link(nc.vector.bn_stats(st[0:n_, l, t, :], src))
                link(nc.vector.bn_aggr(mv[0:n_, l, t, :], st[0:n_, l, t, :]))
                return nc.vector.tensor_scalar_add(ve[0:n_, l, t, 0:1], mv[0:n_, l, t, 1:2], EPS)

            def residual(t):
                n_ = TILES[t][1]
                dve.wait_ge(hb_done, t + 1)
                dve.wait_ge(a_mm, t + 1)
                nc.vector.tensor_tensor(h2[0:n_, t % 2, :], E_BANK[0:n_, 0:E], hb[0:n_, t % 2, :], ALU.add).then_inc(h2_done, 1)
                dve.wait_ge(h2_done, t + 1)
                link(stats(2, t, h2[0:n_, t % 2, :]))
                nc.vector.scalar_tensor_tensor(out=ve[0:n_, 2, t, 1:2], in0=ve[0:n_, 2, t, 0:1], scalar=EPS,
                                               in1=mv[0:n_, 2, t, 1:2], op0=ALU.mult, op1=ALU.add).then_inc(var[2], 1)
                dve.wait_ge(rstd[2], t + 1)
                nc.vector.tensor_scalar(tn[0:n_, t % 2, :], h2[0:n_, t % 2, :], mv[0:n_, 2, t, 0:1], rs[0:n_, 2, t, 1:2],
                                        ALU.subtract, ALU.mult).then_inc(tn_done, 1)

            def embed_stats(t):
                n_ = TILES[t][1]
                dve.wait_ge(emb, t + 1)
                stats(0, t, E_BANK[0:n_, 0:E]).then_inc(var[0], 1)
                nc.vector.scalar_tensor_tensor(out=hg[0:n_, t % 2, :], in0=E_BANK[0:n_, 0:E], scalar=mv[0:n_, 0, t, 0:1],
                                               in1=rowb[0:n_, 0, :], op0=ALU.subtract, op1=ALU.mult).then_inc(hg_done, 1)

            def embed_norm(t):
                n_ = TILES[t][1]
                dve.wait_ge(hg_done, t + 1)
                dve.wait_ge(rstd[0], t + 1)
                nc.vector.scalar_tensor_tensor(out=h1[0:n_, t % 2, :], in0=hg[0:n_, t % 2, :], scalar=rs[0:n_, 0, t, 0:1],
                                               in1=rowb[0:n_, 1, :], op0=ALU.mult, op1=ALU.add).then_inc(h1_done, 1)
                dve.wait_ge(h1_done, t + 1)
                stats(1, t, h1[0:n_, t % 2, :]).then_inc(var[1], 1)

            def attn_norm(t):
                n_ = TILES[t][1]
                dve.wait_ge(rstd[1], t + 1)
                nc.vector.tensor_scalar(x2[0:n_, t % 2, :], h1[0:n_, t % 2, :], mv[0:n_, 1, t, 0:1], rs[0:n_, 1, t, 0:1],
                                        ALU.subtract, ALU.mult).then_inc(x2_done, 1)

            def score_group(t, i):
                c, j, nj = groups(t)[i]
                k, pn = group_at[t] + i, TILES[t][1] // IMGS
                g0 = c * pn + j
                sc = bank[k % 2][:, 0:nj * P].rearrange("p (j w) -> p j w", w=P)[:, :, PADW:P]
                dve.wait_ge(s_mm, k + 1)
                link(nc.vector.tensor_reduce(mx[:, t, g0:g0 + nj], sc, AX, ALU.max))
                nc.vector.tensor_tensor(sd[:, t % 2, g0 * IMGS:(g0 + nj) * IMGS].rearrange("p (g k) -> p g k", k=IMGS), sc,
                                        mx[:, t, g0:g0 + nj].unsqueeze(2).to_broadcast([P, nj, IMGS]),
                                        ALU.subtract).then_inc(s_sub, 1)

            def softmax_end(t):
                gn = KC * (TILES[t][1] // IMGS)
                e3 = ex[:, t % 2, 0:gn * IMGS].rearrange("p (g k) -> p g k", k=IMGS)
                dve.wait_ge(s_exp, t + 1)
                link(nc.vector.tensor_reduce(sm[:, t, 0:gn], e3, AX, ALU.add))
                link(nc.vector.reciprocal(smi[:, t, 0:gn], sm[:, t, 0:gn]))
                nc.vector.tensor_tensor(pr[:, t % 2, 0:gn * IMGS].rearrange("p (g k) -> p g k", k=IMGS), e3,
                                        smi[:, t, 0:gn].unsqueeze(2).to_broadcast([P, gn, IMGS]),
                                        ALU.mult).then_inc(p_done, 1)

            def choose(t):
                n_ = TILES[t][1]
                dve.wait_ge(g_mm, t + 1)
                nc.vector.tensor_copy(g[0:n_, t, :], P_BANK[0:n_, 0:EXPERTS]).then_inc(g_read, 1)
                dve.wait_ge(g_read, t + 1)
                link(nc.vector.max(top[0:n_, t, :], g[0:n_, t, :]))
                nc.vector.tensor_scalar(gd[0:n_, t, :], g[0:n_, t, :], top[0:n_, t, 0:1], None,
                                        ALU.subtract).then_inc(g_sub, 1)
                link(nc.vector.memset(top[0:n_, t, TOPK:8], -3.0e38))
                link(nc.vector.match_replace(rep[0:n_, t, :], top[0:n_, t, :], g[0:n_, t, :], 3.0e38))
                nc.vector.tensor_single_scalar(gmask[0:n_, t, :], rep[0:n_, t, :], 2.9e38, ALU.is_ge).then_inc(gm_done, 1)

            def weigh(t):
                n_ = TILES[t][1]
                dve.wait_ge(gm_done, t + 1)
                dve.wait_ge(g_exp, t + 1)
                link(nc.vector.tensor_tensor(gm[0:n_, t, :], ge[0:n_, t, :], gmask[0:n_, t, :], ALU.mult))
                link(nc.vector.tensor_reduce(gs[0:n_, t:t + 1], gm[0:n_, t, :], AX, ALU.add))
                link(nc.vector.reciprocal(gi[0:n_, t:t + 1], gs[0:n_, t:t + 1]))
                nc.vector.tensor_scalar(route[0:n_, t, :], gm[0:n_, t, :], gi[0:n_, t:t + 1], None,
                                        ALU.mult).then_inc(r_done, 1)

            def spread_p(t):
                n_ = TILES[t][1]
                dve.wait_ge(pt_act, t + 1)
                for j in range(PPT // 2, n_ // IMGS):
                    ins = spread(ptb[0:n_, :, j, :], P_BANK[0:n_, 0:E].rearrange("p (h q) -> p h q", h=HEADS),
                                 mask[0:n_, j:j + 1])
                ins.then_inc(pt_dve, 1)

            def values(t):
                n_ = TILES[t][1]
                dve.wait_ge(v_mm, t + 1)
                nc.vector.scalar_tensor_tensor(out=vs[0:n_, t % 2, PADW:PADW + E], in0=E_BANK[0:n_, 0:E], scalar=dsc[0:n_, 1:2],
                                               in1=rowb[0:n_, 2, :], op0=ALU.mult, op1=ALU.add).then_inc(v_done, 1)

            def spread_q(t):
                at, n_ = TILES[t]
                dve.wait_ge(q_done, t + 1)
                for j in range(HPC):
                    ins = spread(qbd[:, 0, at // IMGS:(at + n_) // IMGS, j, :],
                                 qt[:, t % 2, 0, 0:n_].rearrange("p (n q) -> p n q", q=IMGS), mask[:, j:j + 1])
                ins.then_inc(qbd_dve, 1)

            dve.wait_ge(in_small, 16 * 4)
            for step in range(NT + ROUTE):
                fresh, attn, route_t = in_flight(step)
                if route_t is not None:
                    residual(route_t)
                if fresh is not None:
                    embed_stats(fresh)
                if step == 0:
                    for m in range(2):
                        dve.wait_ge(in_qv, 32)
                        dve.wait_ge(dora_mm, m + 1)
                        nc.vector.tensor_tensor(wqv[:, m, :, :], pw[:, m, :, :],
                                                bank[6 + m][:, 0:KC * E].rearrange("p (k n) -> p k n", k=KC),
                                                ALU.add).then_inc(dora_w, 1)
                count = len(groups(attn)) if attn is not None else 0
                for i in range(0, min(1, count)):
                    score_group(attn, i)
                if fresh is not None:
                    embed_norm(fresh)
                for i in range(1, min(2, count)):
                    score_group(attn, i)
                if fresh is not None:
                    attn_norm(fresh)
                for i in range(2, count):
                    score_group(attn, i)
                if step == 0:
                    dve.wait_ge(dora_sum, 1)
                    nc.vector.tensor_copy(sst[:, :], bank[3][:, 0:2]).then_inc(dora_tot, 1)
                    dve.wait_ge(dora_nrm, 1)
                    link(nc.vector.tensor_scalar_add(nrme[:, :], nrm[:, :], 1e-8))
                    link(nc.vector.reciprocal(nrmi[:, :], nrme[:, :]))
                    nc.vector.tensor_tensor(dsc[:, :], nrmi[:, :], mag[:, :], ALU.mult).then_inc(dora_s, 1)
                    dve.wait_ge(dora_s, 1)
                if route_t is not None:
                    choose(route_t)
                if attn is not None:
                    softmax_end(attn)
                if route_t is not None:
                    weigh(route_t)
                if fresh is not None:
                    spread_q(fresh)
                if attn is not None:
                    spread_p(attn)
                if fresh is not None:
                    values(fresh)

            def biases(s):
                nc.vector.tensor_copy(bb[:, s, 0:2], we[:, s, B1_AT:B1_AT + 2])
                nc.vector.tensor_scalar_add(bb[:, s, 2:4], we[:, s, B1_AT + 2:B1_AT + 4], 1.0).then_inc(bb_done, 1)

            def first(at, u, more):
                b, s, j = u % RING, u // UNITS, (u % UNITS) // 2
                if u % UNITS == 0:
                    dve.wait_ge(bb_done, at * 2 + s + 1)
                dve.wait_ge(up_mm, at * (2 * UNITS) + u + 1)
                nc.vector.tensor_scalar(xg[:, b, :], bank[2 * (u % 2)][:, 0:HALF], bb[:, s, j:j + 1], LIMIT,
                                        ALU.add, ALU.min).then_inc(xg_done, 1)
                if more and u % UNITS == 1:
                    next_in(dve, at, s)
                    biases(1 - s)

            def second(at, u):
                b = u % RING
                dve.wait_ge(sr_done, at * (2 * UNITS) + u + 1)
                nc.vector.tensor_scalar(lc[:, b % 2, :], li[:, b, :], LIMIT + 1, LIMIT + 1, ALU.max, ALU.min)
                nc.vector.tensor_tensor(xs[:, b % 2, :], xg[:, b, :], sr[:, b, :], ALU.mult).then_inc(xs_done, 1)
                dve.wait_ge(xs_done, at * (2 * UNITS) + u + 1)
                nc.vector.tensor_tensor(sw[:, b, :], xs[:, b % 2, :], lc[:, b % 2, :], ALU.mult).then_inc(sw_done, 1)

            def third(at, u):
                dve.wait_ge(hi_done, at * (2 * UNITS) + u + 1)
                nc.vector.tensor_tensor(slo[:, u % RING, :], sw[:, u % RING, :], shi[:, u % RING, :],
                                        ALU.subtract).then_inc(lo_done, 1)

            dve.wait_ge(w_in[0], 16)
            biases(0)
            for u in range(2 * UNITS):
                first(0, u, True)
                if u >= 1:
                    second(0, u - 1)
                if u >= 2:
                    third(0, u - 2)
            with dve.Fori(1, EXPERTS // 2 - 1) as i:
                for u in range(2 * UNITS):
                    first(i, u, True)
                    second(i - 1 if u < 1 else i, (u - 1) % (2 * UNITS))
                    third(i - 1 if u < 2 else i, (u - 2) % (2 * UNITS))
            last = EXPERTS // 2 - 1
            for u in range(2 * UNITS):
                first(last, u, u < UNITS)
                second(last - (u < 1), (u - 1) % (2 * UNITS))
                third(last - (u < 2), (u - 2) % (2 * UNITS))
            third(last, 2 * UNITS - 2)
            second(last, 2 * UNITS - 1)
            third(last, 2 * UNITS - 1)
            dve.wait_ge(down_mm, EXPERTS * UNITS)
            for hf in range(2):
                nc.vector.tensor_copy(res[:, 0, hf * HALF:(hf + 1) * HALF], acc(0, hf)).then_inc(res_dve, 1)

        @block.tensor
        def _(pe):
            mm = nc.tensor.matmul
            pe.wait_ge(in_dora, 16)
            for m in range(2):
                for k in range(KC):
                    ins = mm(bank[6 + m][:, k * E:(k + 1) * E], dr[:, 2 * m, k * P:(k + 1) * P], dr[:, 2 * m + 1, :],
                             start=(k == 0), stop=True, skip_group_check=True)
                ins.then_inc(dora_mm, 1)
            pe.wait_ge(in_add, 32)
            pe.wait_ge(in_w, 16)

            def turn(dst, src, n_, done):
                for c in range(KC):
                    ins = nc.tensor.transpose(dst[:, c * n_:(c + 1) * n_], src[:, c * P:(c + 1) * P], ident[0:n_, 0:n_])
                ins.then_inc(done, 1)

            def embed(t):
                at, n_ = TILES[t]
                pe.wait_ge(in_x[t], 16)
                if t >= ROUTE:
                    pe.wait_ge(h2_done, t - ROUTE + 1)
                elif t:
                    pe.wait_ge(v_done, t)
                o = E_BANK[0:n_, 0:E]
                mm(o, addsel[:, at:at + n_], addr[:, :], start=True, stop=False)
                for k in range(KD):
                    ins = mm(o, xt[:, KD * at + k * n_:KD * at + (k + 1) * n_], wt[:, k, :], start=False, stop=(k == KD - 1))
                ins.then_inc(emb, 1)

            def turn_ffn(t):
                pe.wait_ge(tn_done, t + 1)
                pe.wait_ge(qk_done, min(t + ROUTE, NT))
                turn(Q_BANK, tn[0:TILES[t][1], t % 2, :], TILES[t][1], tt_mm)

            def scores(t):
                pe.wait_ge(qbd_dve, t + 1)
                pe.wait_ge(qbd_pool, t + 1)
                pe.wait_ge(qk_done, t + 1)
                if t == 0:
                    pe.wait_ge(set_up, 4)
                for i, (c, j0, nj) in enumerate(groups(t)):
                    k = group_at[t] + i
                    if k >= 2:
                        pe.wait_ge(s_sub, k - 1)
                    for j in range(nj):
                        pos = t * PPT + j0 + j
                        ins = mm(bank[k % 2][:, j * P:(j + 1) * P], qbd[:, c, pos, :, :].rearrange("p h q -> p (h q)"),
                                 kt[:, c, pos * IMGS:pos * IMGS + P], start=True, stop=True)
                    ins.then_inc(s_mm, 1)

            def turn_attn(t):
                n_ = TILES[t][1]
                pe.wait_ge(x2_done, t + 1)
                if t >= ROUTE:
                    pe.wait_ge(ot_done, t - ROUTE + 1)
                turn(T_BANK, x2[0:n_, t % 2, :], n_, x2t_mm)

            def gate_mm(t):
                at, n_ = TILES[t]
                pe.wait_ge(tt_done, t + 1)
                if t == 0:
                    pe.wait_ge(in_gate, 48)
                o = P_BANK[0:n_, 0:EXPERTS]
                for k in range(KC):
                    mm(o, tt[:, k, at:at + n_], gw[:, k, :], start=(k == 0), stop=False)
                mm(o, ones[0:1, 0:n_], gb[:, :], start=False, stop=True).then_inc(g_mm, 1)

            def queries_keys(t):
                at, n_ = TILES[t]
                pe.wait_ge(x2t_done, t + 1)
                if t == 0:
                    pe.wait_ge(dora_w, 2)
                    pe.wait_ge(in_ko, 32)
                for i, w in enumerate((wqv[:, 0], pw[:, 2])):
                    for c in range(KC):
                        o = (i * KC + c) * P
                        for k in range(KC):
                            ins = mm(Q_BANK[:, o:o + n_], w[:, k, c * P:(c + 1) * P], x2t[:, t % 2, k, 0:n_],
                                     start=(k == 0), stop=(k == KC - 1))
                ins.then_inc(qk_mm, 1)

            def values_mm(t):
                at, n_ = TILES[t]
                pe.wait_ge(hg_done, t + 1)
                for k in range(KC):
                    ins = mm(E_BANK[0:n_, 0:E], x2t[:, t % 2, k, 0:n_], wqv[:, 1, k, :], start=(k == 0), stop=(k == KC - 1))
                ins.then_inc(v_mm, 1)

            def turn_p(t):
                n_ = TILES[t][1]
                pe.wait_ge(p_done, t + 1)
                if t:
                    pe.wait_ge(g_read, t)
                for c in range(KC):
                    ins = nc.tensor.transpose(P_BANK[0:n_, c * P:(c + 1) * P], pr[:, t % 2, c * n_:(c + 1) * n_], ident)
                ins.then_inc(pt_mm, 1)

            def mix(t):
                n_ = TILES[t][1]
                pe.wait_ge(v_done, t + 1)
                pe.wait_ge(pt_act, t + 1)
                pe.wait_ge(pt_dve, t + 1)
                for gi_ in range(V_GROUPS):
                    k = V_GROUPS * t + gi_
                    if k >= 2:
                        pe.wait_ge(o_done, k - 1)
                    for i in range(4):
                        h = 4 * gi_ + i
                        ins = mm(bank[2 + k % 2][0:n_, i * P:(i + 1) * P],
                                 ptb[0:n_, h, 0:n_ // IMGS, :].rearrange("p n q -> p (n q)"),
                                 vs[0:n_, t % 2, h * HD:h * HD + P], start=True, stop=True)
                    ins.then_inc(o_mm, 1)

            def turn_route(t):
                at, n_ = TILES[t]
                pe.wait_ge(r_done, t + 1)
                nc.tensor.transpose(T_BANK[0:EXPERTS, 0:n_], route[0:n_, t, :], ident[0:n_, 0:n_]).then_inc(rt_mm, 1)

            def turn_out(t):
                pe.wait_ge(o_done, V_GROUPS * (t + 1))
                if t:
                    pe.wait_ge(rt_done, t)
                turn(T_BANK, os_[0:TILES[t][1], t % 2, :], TILES[t][1], ot_mm)

            def project(t):
                at, n_ = TILES[t]
                pe.wait_ge(ot_done, t + 1)
                pe.wait_ge(v_done, min(t + 2, NT))
                for k in range(KC):
                    ins = mm(E_BANK[0:n_, 0:E], ot[:, t % 2, k, 0:n_], pw[:, 3, k, :], start=(k == 0), stop=(k == KC - 1))
                ins.then_inc(a_mm, 1)

            for step in range(NT + ROUTE):
                fresh, attn, route_t = in_flight(step)
                if fresh is not None:
                    embed(fresh)
                if step == 0:
                    pe.wait_ge(in_small, 16 * 4)
                if route_t is not None:
                    turn_ffn(route_t)
                if attn is not None:
                    scores(attn)
                if fresh is not None:
                    turn_attn(fresh)
                if step == 0:
                    pe.wait_ge(dora_sq, 2)
                    mm(bank[3][:, 0:2], ones, ss[:, :], start=True, stop=True).then_inc(dora_sum, 1)
                if route_t is not None:
                    gate_mm(route_t)
                if fresh is not None:
                    queries_keys(fresh)
                if attn is not None:
                    turn_p(attn)
                if fresh is not None:
                    values_mm(fresh)
                if route_t is not None:
                    turn_route(route_t)
                if attn is not None:
                    mix(attn)
                    turn_out(attn)
                    project(attn)
            def exact(o, w, x, first, last):
                (w_hi_, w_lo_), (x_hi_, x_lo_) = w, x
                mm(o, w_hi_, x_hi_, start=first, stop=False)
                mm(o, w_hi_, x_lo_, start=False, stop=False)
                return mm(o, w_lo_, x_hi_, start=False, stop=last)

            def up(at, u):
                s, j, hf = u // UNITS, (u % UNITS) // 2, u % 2
                cols = slice(hf * HALF, (hf + 1) * HALF)
                if u % UNITS == 0:
                    pe.wait_ge(w_lo, at * (2 * UNITS) + u + UNITS - 1)
                if not isinstance(at, int) or at * 2 * UNITS + u >= 2:
                    pe.wait_ge(xg_done, at * (2 * UNITS) + u - 1)
                    pe.wait_ge(li_done, at * (2 * UNITS) + u - 1)
                for m in range(2):
                    for k in range(KC):
                        ins = exact(bank[2 * (u % 2) + m][:, 0:HALF],
                                    (w1(whi, s)[:, k, 2 * m + j, :], w1(wlo, s)[:, k, 2 * m + j, :]),
                                    (thi[:, k, cols], tlo[:, k, cols]), k == 0, k == KC - 1)
                ins.then_inc(up_mm, 1)

            def down(at, u, last=False):
                s, j, hf, b = u // UNITS, (u % UNITS) // 2, u % 2, u % RING
                if u % UNITS == 0:
                    pe.wait_ge(w_lo, at * (2 * UNITS) + u + UNITS)
                pe.wait_ge(lo_done, at * (2 * UNITS) + u + 1)
                for c in range(KC):
                    ins = exact(acc(c, hf), (w2(whi, s)[:, j, c, :], w2(wlo, s)[:, j, c, :]),
                                (shi[:, b, :], slo[:, b, :]), False, last)
                ins.then_inc(down_mm, 1)

            pe.wait_ge(tlo_done, NT)
            for u in range(LAG):
                up(0, u)
            pe.wait_ge(rt_done, NT)
            pe.wait_ge(hx_done, NT)
            for c in range(KC):
                for hf in range(2):
                    lo, hi = hf * HALF, (hf + 1) * HALF
                    mm(acc(c, hf), b2s[:, c * P:(c + 1) * P], rt[:, lo:hi], start=True, stop=False)
                    for t, (at, n_) in enumerate(TILES):
                        a, b = max(at, lo), min(at + n_, hi)
                        if a < b:
                            mm(acc(c, hf)[:, a - lo:b - lo], hx[0:n_, t, c * P:(c + 1) * P], ident[0:n_, a - at:b - at],
                               start=False, stop=False)
            with pe.Fori(0, EXPERTS // 2 - 1) as i:
                for u in range(2 * UNITS):
                    down(i, u)
                    if u + LAG < 2 * UNITS:
                        up(i, u + LAG)
                    else:
                        up(i + 1, u + LAG - 2 * UNITS)
            for u in range(2 * UNITS):
                down(EXPERTS // 2 - 1, u, u >= 2 * UNITS - 2)
                if u + LAG < 2 * UNITS:
                    up(EXPERTS // 2 - 1, u + LAG)


def kernel(**inputs):
    import numpy as np
    import concourse.bacc as bacc
    from concourse import mybir as mb
    from concourse.bass_utils import run_bass_kernel_spmd as run

    a = {k: np.asarray(v) for k, v in inputs.items()}
    f = np.float32
    x = a["x"].reshape(IMGS, CH, GRID, PATCH, GRID, PATCH).transpose(1, 3, 5, 2, 4, 0).reshape(D_IN, TOK - IMGS)
    x_t = np.concatenate([np.zeros((D_IN, IMGS), f), x], axis=1)
    add_rows = np.concatenate([a["L0_tok_pos_embedding"][0], a["L0_tok_b"][None], a["L0_tok_cls_token"][0]])
    sel = np.zeros((ADD_ROWS, TOK), f)
    for p in range(POS):
        sel[p, p * IMGS:(p + 1) * IMGS] = 1
    sel[POS, IMGS:] = 1
    sel[POS + 1, :IMGS] = 1

    def col(v):
        return v.reshape(KC, P).T

    w1 = a["L0_ffn_mlp1_w"].reshape(EXPERTS, INNER, 2, KC, P).transpose(0, 4, 3, 2, 1).reshape(EXPERTS, P, -1)
    w2 = a["L0_ffn_mlp2_w"].reshape(EXPERTS, E, KC, P).transpose(0, 3, 2, 1).reshape(EXPERTS, P, -1)
    b1 = a["L0_ffn_mlp1_b"].reshape(EXPERTS, KC, P, 2).transpose(0, 2, 3, 1).reshape(EXPERTS, P, 4)
    consts = np.zeros((P, 2 * P + HPC), f)
    consts[:, :P] = np.eye(P)
    consts[:, P:2 * P] = 1
    consts[np.arange(P), 2 * P + np.arange(P) // HD] = 1
    arrays = {
        "x_t": np.concatenate([x_t[:, at:at + n].reshape(KD, P, n).transpose(1, 0, 2).reshape(P, KD * n) for at, n in TILES], axis=1), "w_tok": a["L0_tok_W"], "add_rows": add_rows, "add_sel": sel,
        "proj": np.stack([a["L0_attn_dir_q"].T, a["L0_attn_dir_v"].T, a["L0_attn_k_w"].T, a["L0_attn_out_w"].T]),
        "dora": np.stack([a["L0_attn_A_q"], a["L0_attn_B_q"].T, a["L0_attn_A_v"], a["L0_attn_B_v"].T], axis=1),
        "rows": np.stack([a["L0_tok_gamma"], a["L0_tok_beta"], a["L0_attn_bias_v"], a["L0_attn_out_b"]]),
        "cols": np.stack([col(a["L0_attn_bias_q"]), col(a["L0_attn_k_b"]), col(a["L0_ffn_scale"])], axis=1),
        "mags": np.stack([a["L0_attn_mag_q"], a["L0_attn_mag_v"]]).reshape(1, 2),
        "gate": a["L0_ffn_gate_w"].T.reshape(KC, P, EXPERTS).transpose(1, 0, 2),
        "gate_b": a["L0_ffn_gate_b"].reshape(1, EXPERTS), "b2": a["L0_ffn_mlp2_b"],
        "experts": np.concatenate([w1, w2, b1], axis=2), "consts": consts,
    }
    arrays = {k: np.ascontiguousarray(v) for k, v in arrays.items()}
    nc = bacc.Bacc("TRN2", target_bir_lowering=False, num_devices=1)
    args = [nc.dram_tensor(f"in_{k}", v.shape, mb.dt.from_np(v.dtype), kind="ExternalInput").ap()
            for k, v in arrays.items()]
    out = nc.dram_tensor("out", [E, TOK], mb.dt.float32, kind="ExternalOutput").ap()
    build(nc, *args, out)
    r = run(nc, [{f"in_{k}": v for k, v in arrays.items()}], core_ids=[0])
    return r.results[0]["out"].reshape(E, POS, IMGS).transpose(2, 1, 0).copy()
```

```python
import concourse.bass as bass
from concourse import mybir
from contextlib import ExitStack

P = 128
IMGS, CH, SIDE, PATCH = 16, 3, 96, 16
GRID = SIDE // PATCH
POS = GRID * GRID + 1
TOK = POS * IMGS
D_IN = CH * PATCH * PATCH
E = 256
HEADS, HD = 16, 16
RANK = 8
EXPERTS, TOPK, INNER = 16, 4, 256
KC = E // P
KD = D_IN // P
PPT = P // IMGS
HPC = P // HD
TILES = [(t * P, min(P, TOK - t * P)) for t in range((TOK + P - 1) // P)]
NT = len(TILES)
HALF = TOK // 2
ADD_ROWS = POS + 2
EPS = 1e-5
ALPHA, LIMIT = 1.702, 7.0

MASK_AT = 2 * P
COL_AT = MASK_AT + HPC
MAG_AT = COL_AT + 3 * KC
GATE_AT = MAG_AT + 2
CONST_COLS = GATE_AT + KC * EXPERTS
WARM = 4
W1_AT, W2_AT = 0, KC * 2 * INNER
B1_AT = W2_AT + KC * E
PIECES = [0, 432, 864, W2_AT, B1_AT]
W_COLS = B1_AT + 4
UNITS = 4
EARLY = (HALF + P - 1) // P
PADW = P - HD
FRESH, QKV, ATTN, ROUTE, TURN = range(5)
RING = 4
LAG = 4


def build(nc, x_t, w_tok, add_rows, add_sel, proj, dora, rows, gate_b, b2, experts, consts, out):
    fp32, fp32r = mybir.dt.float32, mybir.dt.float32r
    ALU = mybir.AluOpType
    ACT = mybir.ActivationFunctionType
    AX = mybir.AxisListType.X

    r_dram = nc.dram_tensor("route_scratch", [EXPERTS, TOK], fp32, kind="Internal").ap()

    with ExitStack() as ctx:
        def sb(name, shape, dt=fp32):
            return ctx.enter_context(nc.sbuf_tensor(name, shape, dt))

        def sem(name):
            return ctx.enter_context(nc.semaphore(name))

        xt = sb("xt", [P, KD * TOK])
        wt = sb("wt", [P, KD, E])
        addr = sb("addr", [ADD_ROWS, E])
        addsel = sb("addsel", [ADD_ROWS, TOK])
        pw = sb("pw", [P, 4, KC, E])
        dr = sb("dr", [RANK, 4, E])
        rowb = sb("rowb", [P, 4, E])
        gb = sb("gb", [1, EXPERTS])
        b2s = sb("b2s", [EXPERTS, E])
        cst = sb("cst", [P, CONST_COLS])
        ident, ones, mask = cst[:, 0:P], cst[:, P:2 * P], cst[:, MASK_AT:COL_AT]
        colb = cst[:, COL_AT:MAG_AT].rearrange("p (m k) -> p m k", m=3)
        mag = cst[:, MAG_AT:GATE_AT]
        gw = cst[:, GATE_AT:CONST_COLS].rearrange("p (k n) -> p k n", k=KC)
        phalf = sb("phalf", [P, 2])

        wqv = sb("wqv", [P, 2, KC, E])
        ss = sb("ss", [P, 2])
        sst = sb("sst", [P, 2])
        nrm = sb("nrm", [P, 2])
        nrme = sb("nrme", [P, 2])
        nrmi = sb("nrmi", [P, 2])
        dsc = sb("dsc", [P, 2])
        st = sb("st", [P, 3, NT, 6])
        mv = sb("mv", [P, 3, NT, 2])
        ve = sb("ve", [P, 3, NT, 2])
        rs = sb("rs", [P, 3, NT, 2])
        ln = sb("ln", [P, 2, E])
        hg = sb("hg", [P, 2, E])
        h1 = sb("h1", [P, 2, E])
        hb = sb("hb", [P, 4, E])
        x2 = sb("x2", [P, 2, E])
        x2t = sb("x2t", [P, 2, KC, P])
        qt = sb("qt", [P, 2, KC, P])
        kt = sb("kt", [P, KC, PADW + TOK])
        qbd = sb("qbd", [P, KC, POS, HPC, IMGS])
        vbd = sb("vbd", [P, KC, HPC * P])
        mx = sb("mx", [P, NT, KC * PPT])
        sd = sb("sd", [P, 2, E])
        ex = sb("ex", [P, 2, E])
        sm = sb("sm", [P, NT, KC * PPT])
        smi = sb("smi", [P, NT, KC * PPT])
        pr = sb("pr", [P, 2, E])
        ptb = sb("ptb", [P, HEADS, PPT, IMGS])
        ot = sb("ot", [P, 2, KC, P])
        h2 = sb("h2", [P, 2, E])
        hx = sb("hx", [P, NT, E])
        tn = sb("tn", [P, 2, E])
        tt = sb("tt", [P, KC, TOK])
        g = sb("g", [P, NT, EXPERTS])
        top = sb("top", [P, NT, 8])
        rep = sb("rep", [P, NT, EXPERTS])
        gmask = sb("gmask", [P, NT, EXPERTS])
        gd = sb("gd", [P, NT, EXPERTS])
        ge = sb("ge", [P, NT, EXPERTS])
        gm = sb("gm", [P, NT, EXPERTS])
        gs = sb("gs", [P, NT])
        gi = sb("gi", [P, NT])
        route = sb("route", [P, NT, EXPERTS])
        rt = sb("rt", [EXPERTS, TOK])
        we = sb("we", [P, 2, W_COLS])
        whi = sb("whi", [P, 2, B1_AT], fp32r)
        wlo = sb("wlo", [P, 2, B1_AT], fp32r)
        thi = sb("thi", [P, KC, TOK], fp32r)
        tlo = sb("tlo", [P, KC, TOK], fp32r)
        shi = sb("shi", [P, RING, HALF], fp32r)
        slo = sb("slo", [P, RING, HALF], fp32r)
        bb = sb("bb", [P, 2, 4])
        rb = sb("rb", [P, 2, TOK])
        ring = qbd[:, :, :, :, :].rearrange("p c n h q -> p (c n h q)")

        def ring_of(at, n):
            return ring[:, at * HALF:(at + n) * HALF].rearrange("p (b n) -> p b n", b=n)

        xg, sg, sr, li, sw = (ring_of(i * RING, RING) for i in range(5))
        lc, xs = ring_of(5 * RING, 2), ring_of(5 * RING + 2, 2)
        res = xt[:, 0:KC * TOK].rearrange("p (k n) -> p k n", k=KC)

        bank = [ctx.enter_context(nc.psum_tensor(f"bank{i}", [P, 512], fp32)) for i in range(8)]

        in_first = [sem(f"in_first{half}") for half in range(2)]
        in_x = [sem(f"in_x{t}") for t in range(NT)]
        in_add, in_dora, in_small, in_gate = (sem(n) for n in ("in_add", "in_dora", "in_small", "in_gate"))
        in_qv, in_ko = sem("in_qv"), sem("in_ko")
        w_in = [sem(f"w_in{s}") for s in range(2)]
        rb_in = [[sem(f"rb_in{s}_half{hf}") for hf in range(2)] for s in range(2)]
        r_out, y_out = sem("r_out"), sem("y_out")
        dve_c, set_up, zeros = (sem(n) for n in ("dve_chain", "set_up", "zeros"))
        dora_mm, dora_w, dora_sq, dora_sum, dora_tot, dora_nrm, dora_s = (
            sem(n) for n in ("dora_mm", "dora_w", "dora_sq", "dora_sum", "dora_tot", "dora_nrm", "dora_s"))
        emb, hg_done, h1_done, hb_done = (sem(n) for n in ("emb", "hg_done", "h1_done", "hb_done"))
        var = [sem(f"var{i}") for i in range(3)]
        rstd = [sem(f"rstd{i}") for i in range(3)]
        x2_done, x2t_mm, x2t_done = (sem(n) for n in ("x2_done", "x2t_mm", "x2t_done"))
        qk_mm, q_done, qk_done, qbd_dve, qbd_pool = (
            sem(n) for n in ("qk_mm", "q_done", "qk_done", "qbd_dve", "qbd_pool"))
        v_mm, v_done = sem("v_mm"), sem("v_done")
        s_mm, s_sub, s_exp, p_done = (sem(n) for n in ("s_mm", "s_sub", "s_exp", "p_done"))
        pt_mm, pt_act, pt_dve = (sem(n) for n in ("pt_mm", "pt_act", "pt_dve"))
        o_mm, ot_done = sem("o_mm"), sem("ot_done")
        a_mm, h2_done, h2_stats, hx_done, ln_done, tn_done, tt_mm, tt_done = (
            sem(n) for n in ("a_mm", "h2_done", "h2_stats", "hx_done", "ln_done", "tn_done", "tt_mm", "tt_done"))
        thi_done, tlo_done = sem("thi_done"), sem("tlo_done")
        g_mm, g_read, g_sub, gm_done, g_exp, r_done, rt_mm, rt_done, rb_mm = (
            sem(n) for n in ("g_mm", "g_read", "g_sub", "gm_done", "g_exp", "r_done", "rt_mm", "rt_done", "rb_mm"))
        w_hi, w_lo, bb_done = (sem(n) for n in ("w_hi", "w_lo", "bb_done"))
        up_mm, xg_done, li_done, sg_done, sr_done, xs_done, sw_done, hi_done, lo_done = (
            sem(n) for n in ("up_mm", "xg_done", "li_done", "sg_done", "sr_done", "xs_done", "sw_done", "hi_done",
                             "lo_done"))
        sum_done = [sem(f"sum_done{c}") for c in range(KC)]
        res_dve, res_act = sem("res_dve"), sem("res_act")

        def acc(c, hf):
            return bank[4 + 2 * c + hf][:, 0:HALF]

        def in_flight(step):
            return [step - lag if 0 <= step - lag < NT else None for lag in (FRESH, QKV, ATTN, ROUTE, TURN)]

        def groups(t):
            pn = TILES[t][1] // IMGS
            return [(c, j, min(4, pn - j)) for c in range(KC) for j in range(0, pn, 4)]

        group_at = [sum(len(groups(i)) for i in range(t)) for t in range(NT + 1)]
        O_BANK = bank[2]
        A_BANK = bank[3]
        E_BANK = bank[4]
        T_BANK = bank[5]
        Q_BANK = bank[6]
        P_BANK = bank[7]

        def projection(t):
            return (A_BANK if t < NT - 1 else bank[1])[0:TILES[t][1], 0:E]

        def w1(w, s):
            return w[:, s, W1_AT:W2_AT].rearrange("p (k m i) -> p k m i", k=KC, m=4)

        def w2(w, s):
            return w[:, s, W2_AT:B1_AT].rearrange("p (k m i) -> p k m i", k=KC, m=KC)

        def next_in(eng, at, s):
            eng.wait_ge(w_in[1 - s], 16 * (at + 1 + s))

        block = ctx.enter_context(nc.Block())

        @block.sync
        def _(sp):
            psrc = proj.rearrange("m (k p) n -> p m k n", p=P)
            wsrc = w_tok.rearrange("(k p) n -> p k n", p=P)

            def load_tile(t, k0, k1, done):
                at, n_ = TILES[t]
                cols = slice(KD * at + k0 * n_, KD * at + k1 * n_)
                sp.dma_start(xt[:, cols], x_t[:, cols]).then_inc(done, 16)

            for half in range(2):
                k0, k1 = half * KD // 2, (half + 1) * KD // 2
                sp.dma_start(wt[:, k0:k1, :], wsrc[:, k0:k1, :]).then_inc(in_first[half], 16)
                load_tile(0, k0, k1, in_first[half])
            for m in range(2):
                sp.dma_start(pw[:, m], psrc[:, m]).then_inc(in_qv, 16)
            load_tile(1, 0, KD, in_x[1])
            for m in range(2, 4):
                sp.dma_start(pw[:, m], psrc[:, m]).then_inc(in_ko, 16)
            for t in range(2, NT):
                load_tile(t, 0, KD, in_x[t])

            def load_expert(e, s):
                sp.dma_start(we[:, s, :], experts[bass.ds(e, 1), :, :].rearrange("a p n -> (a p) n")).then_inc(w_in[s], 16)

            def load_route(e, s, hf):
                cols = slice(hf * HALF, (hf + 1) * HALF)
                sp.dma_start(rb[:, s, cols], r_dram[bass.ds(e, 1), cols].to_broadcast([P, HALF])).then_inc(rb_in[s][hf], 16)

            for s in range(2):
                load_expert(s, s)
            for hf in range(2):
                cols = slice(hf * HALF, (hf + 1) * HALF)
                sp.wait_ge(rt_done, (EARLY, NT)[hf])
                sp.dma_start(r_dram[:, cols], rt[:, cols]).then_inc(r_out, 16)
                sp.wait_ge(r_out, 16 * (hf + 1))
                for s in range(hf, 2):
                    load_route(s, s, hf)
            with sp.Fori(1, EXPERTS // 2) as i:
                for s in range(2):
                    sp.wait_ge(w_lo, i * (2 * UNITS) + UNITS * (s - 1))
                    sp.wait_ge(bb_done, i * 2 + s - 1)
                    load_expert(i * 2 + s, s)
                    sp.wait_ge(sr_done, i * (2 * UNITS) + UNITS * (s - 1))
                    for hf in range(2):
                        load_route(i * 2 + s, s, hf)
            for hf in range(2):
                cols = slice(hf * HALF, (hf + 1) * HALF)
                for c, copied in enumerate((res_dve, res_act)):
                    sp.wait_ge(copied, hf + 1)
                    sp.dma_start(out[c * P:(c + 1) * P, cols], res[:, c, cols]).then_inc(y_out, 16)
            sp.wait_ge(y_out, 16 * 2 * KC)

        @block.gpsimd
        def _(pool):
            for dst, value in ((phalf[:, 0:1], -0.5), (phalf[:, 1:2], 0.5), (kt[:, :, 0:PADW], 0.0), (vbd[:, :, :], 0.0)):
                nc.gpsimd.memset(dst, value).then_inc(set_up, 1)
            pool.wait_ge(set_up, 4)

            def inv_root(l, t, w):
                n_ = TILES[t][1]
                pool.wait_ge(var[l], t + 1)
                nc.gpsimd.tensor_tensor(rs[0:n_, l, t, 0:w], ve[0:n_, l, t, 0:w], phalf[0:n_, 0:1].to_broadcast([n_, w]),
                                        ALU.pow).then_inc(rstd[l], 1)

            def sum_base(t):
                n_ = TILES[t][1]
                pool.wait_ge(ln_done, t + 1)
                nc.gpsimd.tensor_tensor(hx[0:n_, t, :], h2[0:n_, t % 2, :], ln[0:n_, t % 2, :], ALU.add).then_inc(hx_done, 1)

            def split_tokens(t):
                at, n_ = TILES[t]
                pool.wait_ge(thi_done, t + 1)
                nc.gpsimd.tensor_tensor(tlo[:, :, at:at + n_], tt[:, :, at:at + n_], thi[:, :, at:at + n_],
                                        ALU.subtract).then_inc(tlo_done, 1)

            def add_out_b(t):
                n_ = TILES[t][1]
                pool.wait_ge(h1_done, t + 1)
                nc.gpsimd.tensor_tensor(hb[0:n_, t % 4, :], h1[0:n_, t % 2, :], rowb[0:n_, 3, :], ALU.add).then_inc(hb_done, 1)

            def spread_q(t):
                at, n_ = TILES[t]
                pn, pos = n_ // IMGS, at // IMGS
                pool.wait_ge(q_done, t + 1)
                nc.gpsimd.tensor_tensor(
                    qbd[:, 1, pos:pos + pn, :, :],
                    qt[:, t % 2, 1, 0:n_].rearrange("p (n q) -> p n q", q=IMGS).unsqueeze(2).to_broadcast([P, pn, HPC, IMGS]),
                    mask.unsqueeze(1).unsqueeze(3).to_broadcast([P, pn, HPC, IMGS]), ALU.mult).then_inc(qbd_pool, 1)

            def split_lo(s, j, n):
                pool.wait_ge(w_hi, n)
                a, b = PIECES[j], PIECES[j + 1]
                nc.gpsimd.tensor_tensor(wlo[:, s, a:b], we[:, s, a:b], whi[:, s, a:b], ALU.subtract).then_inc(w_lo, 1)

            inv_root(0, 0, 1)
            inv_root(1, 0, 1)
            add_out_b(0)
            inv_root(0, 1, 1)
            pool.wait_ge(dora_tot, 1)
            nc.gpsimd.tensor_tensor(nrm[:, :], sst[:, :], phalf[:, 1:2].to_broadcast([P, 2]), ALU.pow).then_inc(dora_nrm, 1)
            inv_root(1, 1, 1)
            spread_q(0)
            add_out_b(1)
            for step in range(ATTN, NT + ATTN):
                fresh, qkv, _, route_t, _ = in_flight(step)
                if route_t is not None:
                    inv_root(2, route_t, 2)
                    split_tokens(route_t)
                if fresh is not None:
                    inv_root(0, fresh, 1)
                if qkv is not None:
                    spread_q(qkv)
                if fresh is not None:
                    inv_root(1, fresh, 1)
                    add_out_b(fresh)
                if route_t is not None:
                    sum_base(route_t)
                if step < ATTN + UNITS:
                    split_lo(0, step - ATTN, step - ATTN + 1)
            def unit(at, u, split):
                b, s, hf = u % RING, u // UNITS, (u % UNITS) // 2
                if u % 2 == 0:
                    pool.wait_ge(rb_in[s][hf], (at + 1) * 16)
                pool.wait_ge(sg_done, at * (2 * UNITS) + u + 1)
                nc.gpsimd.tensor_tensor(sr[:, b, :], sg[:, b, :], rb[:, s, hf * HALF:(hf + 1) * HALF],
                                        ALU.mult).then_inc(sr_done, 1)
                if split:
                    split_lo(1 - s, u % UNITS, at * (2 * UNITS) + u + UNITS + 1)

            unit(0, 0, True)
            inv_root(2, NT - 1, 2)
            split_lo(1, 1, UNITS + 2)
            split_tokens(NT - 1)
            sum_base(NT - 1)
            unit(0, 1, False)
            split_lo(1, 2, UNITS + 3)
            for u in range(2, 2 * UNITS):
                unit(0, u, u > 2)
            with pool.Fori(1, EXPERTS // 2 - 1) as i:
                for u in range(2 * UNITS):
                    unit(i, u, True)
            for u in range(2 * UNITS):
                unit(EXPERTS // 2 - 1, u, u < UNITS)

        @block.scalar
        def _(act):
            for dst, src in ((addr, add_rows), (addsel, add_sel)):
                act.dma_start(dst[:, :], src).then_inc(in_add, 16)
            act.dma_start(rowb[:, :, :], rows.rearrange("(a m) n -> a m n", a=1).to_broadcast([P, 4, E])).then_inc(in_small, 16)
            act.dma_start(dr[:, :, :], dora).then_inc(in_dora, 16)
            act.dma_start(cst[:, :], consts).then_inc(in_small, 16)
            act.dma_start(gb[:, :], gate_b).then_inc(in_gate, 16)
            act.dma_start(b2s[:, :], b2).then_inc(in_gate, 16)
            for m in range(2):
                act.wait_ge(dora_w, m + 1)
                if m:
                    act.wait_ge(dora_sq, 1)
                nc.scalar.activation(ex[:, :, :].rearrange("p k n -> p (k n)"),
                                     wqv[:, m, :, :].rearrange("p k n -> p (k n)"), ACT.Square,
                                     accum_out=ss[:, m:m + 1]).then_inc(dora_sq, 1)
            act.wait_ge(in_small, 16 * 2)

            def copy_route(t):
                at, n_ = TILES[t]
                act.wait_ge(rt_mm, t + 1)
                nc.scalar.copy(rt[:, at:at + n_], P_BANK[0:EXPERTS, 0:n_]).then_inc(rt_done, 1)

            def exp_scores(t):
                w = KC * TILES[t][1]
                act.wait_ge(s_sub, group_at[t + 1])
                nc.scalar.activation(ex[:, t % 2, 0:w], sd[:, t % 2, 0:w], ACT.Exp, scale=HD ** -0.5).then_inc(s_exp, 1)

            def scale_tokens(t):
                at, n_ = TILES[t]
                act.wait_ge(tt_mm, t + 1)
                for c in range(KC):
                    ins = nc.scalar.activation(tt[:, c, at:at + n_], T_BANK[:, c * n_:(c + 1) * n_], ACT.Copy,
                                               scale=colb[:, 2, c:c + 1])
                ins.then_inc(tt_done, 1)
                for c in range(KC):
                    ins = nc.scalar.activation(thi[:, c, at:at + n_], T_BANK[:, c * n_:(c + 1) * n_], ACT.Copy,
                                               scale=colb[:, 2, c:c + 1])
                ins.then_inc(thi_done, 1)

            def spread_p(t):
                n_ = TILES[t][1]
                act.wait_ge(pt_mm, t + 1)
                if t:
                    act.wait_ge(o_mm, t)
                for j in range(n_ // IMGS):
                    ins = nc.scalar.activation(ptb[0:n_, 0:HPC, j, :], P_BANK[0:n_, 0:P].rearrange("p (h q) -> p h q", h=HPC),
                                               ACT.Copy, scale=mask[0:n_, j:j + 1])
                ins.then_inc(pt_act, 1)

            def bias_qk(t):
                at, n_ = TILES[t]
                act.wait_ge(dora_s, 1)
                act.wait_ge(qk_mm, t + 1)
                if t >= 2:
                    act.wait_ge(qbd_dve, t - 1)
                    act.wait_ge(qbd_pool, t - 1)
                for c in range(KC):
                    ins = nc.scalar.activation(qt[:, t % 2, c, 0:n_], Q_BANK[:, c * P:c * P + n_], ACT.Identity,
                                               bias=colb[:, 0, c:c + 1], scale=dsc[:, 0:1])
                ins.then_inc(q_done, 1)
                for c in range(KC):
                    ins = nc.scalar.activation(kt[:, c, PADW + at:PADW + at + n_],
                                               Q_BANK[:, (KC + c) * P:(KC + c) * P + n_], ACT.Identity,
                                               bias=colb[:, 1, c:c + 1])
                ins.then_inc(qk_done, 1)

            def copy_out(t):
                n_ = TILES[t][1]
                act.wait_ge(o_mm, t + 1)
                nc.scalar.copy(ot[:, t % 2, :, 0:n_], O_BANK[:, 0:KC * P].rearrange("p (k n) -> p k n", k=KC)[:, :, 0:n_]
                               ).then_inc(ot_done, 1)

            def copy_normed(t):
                n_ = TILES[t][1]
                act.wait_ge(x2t_mm, t + 1)
                nc.scalar.copy(x2t[:, t % 2, :, 0:n_], T_BANK[:, 0:KC * n_].rearrange("p (k n) -> p k n", k=KC)
                               ).then_inc(x2t_done, 1)

            def exp_gate(t):
                n_ = TILES[t][1]
                act.wait_ge(g_sub, t + 1)
                nc.scalar.activation(ge[0:n_, t, :], gd[0:n_, t, :], ACT.Exp).then_inc(g_exp, 1)

            def split_hi(s, j):
                a, b = PIECES[j], PIECES[j + 1]
                nc.scalar.copy(whi[:, s, a:b], we[:, s, a:b]).then_inc(w_hi, 1)

            def lin(at, u):
                b, s, j = u % RING, u // UNITS, u % 2
                if u % UNITS == 0:
                    act.wait_ge(bb_done, at * 2 + s + 1)
                act.wait_ge(up_mm, at * (2 * UNITS) + u + 1)
                nc.scalar.activation(li[:, b, :], bank[2 * (u % 2) + 1][:, 0:HALF], ACT.Identity,
                                     bias=bb[:, s, 2 + j:3 + j]).then_inc(li_done, 1)

            def sigmoid(at, u, split):
                b, s = u % RING, u // UNITS
                act.wait_ge(xg_done, at * (2 * UNITS) + u + 1)
                nc.scalar.activation(sg[:, b, :], xg[:, b, :], ACT.Sigmoid, scale=ALPHA).then_inc(sg_done, 1)
                if split:
                    if u % UNITS == 0:
                        next_in(act, at, s)
                    split_hi(1 - s, u % UNITS)

            def round_s(at, u):
                act.wait_ge(sw_done, at * (2 * UNITS) + u + 1)
                nc.scalar.copy(shi[:, u % RING, :], sw[:, u % RING, :]).then_inc(hi_done, 1)

            copy_normed(0)
            bias_qk(0)
            copy_normed(1)
            for step in range(ATTN, NT + ATTN):
                fresh, qkv, attn, route_t, turned = in_flight(step)
                if turned is not None:
                    copy_route(turned)
                exp_scores(attn)
                if route_t is not None:
                    scale_tokens(route_t)
                spread_p(attn)
                if attn == NT - 2:
                    lin(0, 0)
                if qkv is not None:
                    bias_qk(qkv)
                if route_t is not None:
                    exp_gate(route_t)
                if qkv is None:
                    sigmoid(0, 0, True)
                copy_out(attn)
                if qkv is None:
                    copy_route(route_t)
                if fresh is not None:
                    copy_normed(fresh)
                if step < ATTN + UNITS:
                    if step == ATTN:
                        act.wait_ge(w_in[0], 16)
                    split_hi(0, step - ATTN)
            round_s(0, 0)
            nc.scalar.activation(ge[0:1, NT - 1, 0:1], gd[0:1, 0, 0:1], ACT.Exp)
            lin(0, 1)
            split_hi(1, 1)
            scale_tokens(NT - 1)
            exp_gate(NT - 1)
            sigmoid(0, 1, False)
            copy_route(NT - 1)
            split_hi(1, 2)
            act.wait_ge(rb_mm, 1)
            nc.scalar.copy(rb[:, 0, HALF:TOK], T_BANK[:, 0:HALF]).then_inc(rb_in[0][1], 16)
            for u in range(2, 2 * UNITS):
                lin(0, u)
                sigmoid(0, u, u > 2)
                round_s(0, u - 1)
            with act.Fori(1, EXPERTS // 2 - 1) as i:
                for u in range(2 * UNITS):
                    lin(i, u)
                    sigmoid(i, u, True)
                    round_s(i - 1 if u == 0 else i, (u - 1) % (2 * UNITS))
            for u in range(2 * UNITS):
                lin(EXPERTS // 2 - 1, u)
                sigmoid(EXPERTS // 2 - 1, u, u < UNITS)
                round_s(EXPERTS // 2 - (2 if u == 0 else 1), (u - 1) % (2 * UNITS))
            round_s(EXPERTS // 2 - 1, 2 * UNITS - 1)
            for hf in range(2):
                act.wait_ge(sum_done[1], hf + 1)
                nc.scalar.copy(res[:, 1, hf * HALF:(hf + 1) * HALF], acc(1, hf)).then_inc(res_act, 1)

        @block.vector
        def _(dve):
            n = [0]

            def link(ins):
                n[0] += 1
                ins.then_inc(dve_c, 1)
                dve.wait_ge(dve_c, n[0])

            def stats(l, t, src):
                link(nc.vector.bn_stats(st[0:TILES[t][1], l, t, :], src))
                return moments(l, t)

            def moments(l, t):
                n_ = TILES[t][1]
                link(nc.vector.bn_aggr(mv[0:n_, l, t, :], st[0:n_, l, t, :]))
                return nc.vector.tensor_scalar_add(ve[0:n_, l, t, 0:1], mv[0:n_, l, t, 1:2], EPS)

            def residual(t):
                n_ = TILES[t][1]
                dve.wait_ge(hb_done, t + 1)
                dve.wait_ge(a_mm, t + 1)
                nc.vector.tensor_tensor(h2[0:n_, t % 2, :], projection(t), hb[0:n_, t % 4, :], ALU.add).then_inc(h2_done, 1)
                dve.wait_ge(h2_done, t + 1)
                nc.vector.bn_stats(st[0:n_, 2, t, :], h2[0:n_, t % 2, :]).then_inc(h2_stats, 1)

            def residual_moments(t):
                n_ = TILES[t][1]
                dve.wait_ge(h2_stats, t + 1)
                moments(2, t)
                nc.vector.tensor_scalar(ve[0:n_, 2, t, 1:2], mv[0:n_, 2, t, 1:2], 1 + EPS, EPS * EPS,
                                        ALU.mult, ALU.add).then_inc(var[2], 1)

            def ffn_norm(t):
                n_ = TILES[t][1]
                dve.wait_ge(rstd[2], t + 1)
                nc.vector.tensor_scalar(tn[0:n_, t % 2, :], h2[0:n_, t % 2, :], mv[0:n_, 2, t, 0:1], rs[0:n_, 2, t, 1:2],
                                        ALU.subtract, ALU.mult).then_inc(tn_done, 1)

            def residual_norm(t):
                n_ = TILES[t][1]
                nc.vector.tensor_scalar(ln[0:n_, t % 2, :], h2[0:n_, t % 2, :], mv[0:n_, 2, t, 0:1], rs[0:n_, 2, t, 0:1],
                                        ALU.subtract, ALU.mult).then_inc(ln_done, 1)

            def embed_stats(t):
                n_ = TILES[t][1]
                dve.wait_ge(emb, t + 1)
                stats(0, t, E_BANK[0:n_, 0:E]).then_inc(var[0], 1)
                nc.vector.scalar_tensor_tensor(out=hg[0:n_, t % 2, :], in0=E_BANK[0:n_, 0:E], scalar=mv[0:n_, 0, t, 0:1],
                                               in1=rowb[0:n_, 0, :], op0=ALU.subtract, op1=ALU.mult).then_inc(hg_done, 1)

            def embed_norm(t):
                n_ = TILES[t][1]
                dve.wait_ge(hg_done, t + 1)
                dve.wait_ge(rstd[0], t + 1)
                nc.vector.scalar_tensor_tensor(out=h1[0:n_, t % 2, :], in0=hg[0:n_, t % 2, :], scalar=rs[0:n_, 0, t, 0:1],
                                               in1=rowb[0:n_, 1, :], op0=ALU.mult, op1=ALU.add).then_inc(h1_done, 1)
                dve.wait_ge(h1_done, t + 1)
                stats(1, t, h1[0:n_, t % 2, :]).then_inc(var[1], 1)

            def attn_norm(t):
                n_ = TILES[t][1]
                dve.wait_ge(rstd[1], t + 1)
                nc.vector.tensor_scalar(x2[0:n_, t % 2, :], h1[0:n_, t % 2, :], mv[0:n_, 1, t, 0:1], rs[0:n_, 1, t, 0:1],
                                        ALU.subtract, ALU.mult).then_inc(x2_done, 1)

            def score_group(t, i):
                c, j, nj = groups(t)[i]
                k, pn = group_at[t] + i, TILES[t][1] // IMGS
                g0 = c * pn + j
                sc = bank[k % 2][:, 0:nj * P].rearrange("p (j w) -> p j w", w=P)[:, :, PADW:P]
                dve.wait_ge(s_mm, k + 1)
                link(nc.vector.tensor_reduce(mx[:, t, g0:g0 + nj], sc, AX, ALU.max))
                nc.vector.tensor_tensor(sd[:, t % 2, g0 * IMGS:(g0 + nj) * IMGS].rearrange("p (g k) -> p g k", k=IMGS), sc,
                                        mx[:, t, g0:g0 + nj].unsqueeze(2).to_broadcast([P, nj, IMGS]),
                                        ALU.subtract).then_inc(s_sub, 1)

            def softmax_end(t):
                gn = KC * (TILES[t][1] // IMGS)
                e3 = ex[:, t % 2, 0:gn * IMGS].rearrange("p (g k) -> p g k", k=IMGS)
                dve.wait_ge(s_exp, t + 1)
                link(nc.vector.tensor_reduce(sm[:, t, 0:gn], e3, AX, ALU.add))
                link(nc.vector.reciprocal(smi[:, t, 0:gn], sm[:, t, 0:gn]))
                nc.vector.tensor_tensor(pr[:, t % 2, 0:gn * IMGS].rearrange("p (g k) -> p g k", k=IMGS), e3,
                                        smi[:, t, 0:gn].unsqueeze(2).to_broadcast([P, gn, IMGS]),
                                        ALU.mult).then_inc(p_done, 1)

            def choose(t):
                n_ = TILES[t][1]
                dve.wait_ge(g_mm, t + 1)
                nc.vector.tensor_copy(g[0:n_, t, :], P_BANK[0:n_, 0:EXPERTS]).then_inc(g_read, 1)
                dve.wait_ge(g_read, t + 1)
                link(nc.vector.max(top[0:n_, t, :], g[0:n_, t, :]))
                nc.vector.tensor_scalar(gd[0:n_, t, :], g[0:n_, t, :], top[0:n_, t, 0:1], None,
                                        ALU.subtract).then_inc(g_sub, 1)
                link(nc.vector.memset(top[0:n_, t, TOPK:8], -3.0e38))
                link(nc.vector.match_replace(rep[0:n_, t, :], top[0:n_, t, :], g[0:n_, t, :], 3.0e38))
                nc.vector.tensor_single_scalar(gmask[0:n_, t, :], rep[0:n_, t, :], 2.9e38, ALU.is_ge).then_inc(gm_done, 1)

            def weigh(t):
                n_ = TILES[t][1]
                dve.wait_ge(gm_done, t + 1)
                dve.wait_ge(g_exp, t + 1)
                link(nc.vector.tensor_tensor(gm[0:n_, t, :], ge[0:n_, t, :], gmask[0:n_, t, :], ALU.mult))
                link(nc.vector.tensor_reduce(gs[0:n_, t:t + 1], gm[0:n_, t, :], AX, ALU.add))
                link(nc.vector.reciprocal(gi[0:n_, t:t + 1], gs[0:n_, t:t + 1]))
                nc.vector.tensor_scalar(route[0:n_, t, :], gm[0:n_, t, :], gi[0:n_, t:t + 1], None,
                                        ALU.mult).then_inc(r_done, 1)

            def spread_p(t):
                n_ = TILES[t][1]
                pn = n_ // IMGS
                dve.wait_ge(pt_mm, t + 1)
                nc.vector.tensor_tensor(
                    ptb[0:n_, HPC:HEADS, 0:pn, :],
                    A_BANK[0:n_, 0:P].rearrange("p (h q) -> p h q", h=HPC).unsqueeze(2).to_broadcast([n_, HPC, pn, IMGS]),
                    mask[0:n_, 0:pn].unsqueeze(1).unsqueeze(3).to_broadcast([n_, HPC, pn, IMGS]), ALU.mult).then_inc(pt_dve, 1)

            def own_columns(c, n_):
                flat = vbd[0:n_, c, :]
                return bass.AP(flat.tensor, flat.offset, [list(flat.ap[0]), [P + HD, HPC], [1, HD]])

            def values(t):
                n_ = TILES[t][1]
                dve.wait_ge(v_mm, t + 1)
                if t:
                    dve.wait_ge(o_mm, t)
                for c in range(KC):
                    ins = nc.vector.scalar_tensor_tensor(
                        out=own_columns(c, n_),
                        in0=E_BANK[0:n_, c * P:(c + 1) * P].rearrange("p (h d) -> p h d", h=HPC), scalar=dsc[0:n_, 1:2],
                        in1=rowb[0:n_, 2, c * P:(c + 1) * P].rearrange("p (h d) -> p h d", h=HPC), op0=ALU.mult, op1=ALU.add)
                ins.then_inc(v_done, 1)

            def spread_q(t):
                at, n_ = TILES[t]
                pn, pos = n_ // IMGS, at // IMGS
                dve.wait_ge(q_done, t + 1)
                nc.vector.tensor_tensor(
                    qbd[:, 0, pos:pos + pn, :, :],
                    qt[:, t % 2, 0, 0:n_].rearrange("p (n q) -> p n q", q=IMGS).unsqueeze(2).to_broadcast([P, pn, HPC, IMGS]),
                    mask.unsqueeze(1).unsqueeze(3).to_broadcast([P, pn, HPC, IMGS]), ALU.mult).then_inc(qbd_dve, 1)

            def biases(s):
                nc.vector.tensor_copy(bb[:, s, 0:2], we[:, s, B1_AT:B1_AT + 2])
                nc.vector.tensor_scalar_add(bb[:, s, 2:4], we[:, s, B1_AT + 2:B1_AT + 4], 1.0).then_inc(bb_done, 1)

            def first(at, u, more):
                b, s, j = u % RING, u // UNITS, u % 2
                if u % UNITS == 0:
                    dve.wait_ge(bb_done, at * 2 + s + 1)
                dve.wait_ge(up_mm, at * (2 * UNITS) + u + 1)
                nc.vector.tensor_scalar(xg[:, b, :], bank[2 * (u % 2)][:, 0:HALF], bb[:, s, j:j + 1], LIMIT,
                                        ALU.add, ALU.min).then_inc(xg_done, 1)
                if more and u % UNITS == 1:
                    next_in(dve, at, s)
                    biases(1 - s)

            def second(at, u):
                b = u % RING
                dve.wait_ge(sr_done, at * (2 * UNITS) + u + 1)
                nc.vector.tensor_scalar(lc[:, b % 2, :], li[:, b, :], LIMIT + 1, LIMIT + 1, ALU.max, ALU.min)
                nc.vector.tensor_tensor(xs[:, b % 2, :], xg[:, b, :], sr[:, b, :], ALU.mult).then_inc(xs_done, 1)
                dve.wait_ge(xs_done, at * (2 * UNITS) + u + 1)
                nc.vector.tensor_tensor(sw[:, b, :], xs[:, b % 2, :], lc[:, b % 2, :], ALU.mult).then_inc(sw_done, 1)

            def third(at, u):
                dve.wait_ge(hi_done, at * (2 * UNITS) + u + 1)
                nc.vector.tensor_tensor(slo[:, u % RING, :], sw[:, u % RING, :], shi[:, u % RING, :],
                                        ALU.subtract).then_inc(lo_done, 1)

            nc.vector.memset(ex[:, :, :], 0.0).then_inc(zeros, 1)
            dve.wait_ge(in_small, 16 * 2)
            dve.wait_ge(set_up, 4)
            embed_stats(0)
            embed_norm(0)
            for m in range(2):
                dve.wait_ge(in_qv, 32)
                dve.wait_ge(dora_mm, m + 1)
                nc.vector.tensor_tensor(wqv[:, m, :, :], pw[:, m, :, :],
                                        bank[6 + m][:, 0:KC * E].rearrange("p (k n) -> p k n", k=KC),
                                        ALU.add).then_inc(dora_w, 1)
            attn_norm(0)
            embed_stats(1)
            dve.wait_ge(dora_sum, 1)
            nc.vector.tensor_copy(sst[:, :], A_BANK[:, 0:2]).then_inc(dora_tot, 1)
            embed_norm(1)
            dve.wait_ge(dora_nrm, 1)
            link(nc.vector.tensor_scalar_add(nrme[:, :], nrm[:, :], 1e-8))
            link(nc.vector.reciprocal(nrmi[:, :], nrme[:, :]))
            nc.vector.tensor_tensor(dsc[:, :], nrmi[:, :], mag[:, :], ALU.mult).then_inc(dora_s, 1)
            dve.wait_ge(dora_s, 1)
            values(0)
            spread_q(0)
            attn_norm(1)
            score_group(0, 0)
            for step in range(ATTN, NT + ATTN):
                fresh, qkv, attn, route_t, _ = in_flight(step)
                if route_t is not None:
                    residual(route_t)
                score_group(attn, 1)
                if route_t is not None:
                    residual_moments(route_t)
                    ffn_norm(route_t)
                for i in range(2, len(groups(attn))):
                    score_group(attn, i)
                softmax_end(attn)
                if fresh is not None:
                    embed_stats(fresh)
                spread_p(attn)
                if attn == NT - 2:
                    dve.wait_ge(w_in[0], 16)
                    biases(0)
                    first(0, 0, True)
                if fresh is not None:
                    embed_norm(fresh)
                if qkv is not None:
                    spread_q(qkv)
                if fresh is not None:
                    attn_norm(fresh)
                if route_t is not None:
                    residual_norm(route_t)
                    choose(route_t)
                    weigh(route_t)
                if qkv is not None:
                    values(qkv)
                    score_group(qkv, 0)
            second(0, 0)
            residual(NT - 1)
            residual_moments(NT - 1)
            third(0, 0)
            ffn_norm(NT - 1)
            first(0, 1, True)
            residual_norm(NT - 1)
            choose(NT - 1)
            weigh(NT - 1)
            for u in range(2, 2 * UNITS):
                first(0, u, True)
                if u > 2:
                    third(0, u - 2)
                second(0, u - 1)
            with dve.Fori(1, EXPERTS // 2 - 1) as i:
                for u in range(2 * UNITS):
                    first(i, u, True)
                    third(i - 1 if u < 2 else i, (u - 2) % (2 * UNITS))
                    second(i - 1 if u < 1 else i, (u - 1) % (2 * UNITS))
            last = EXPERTS // 2 - 1
            for u in range(2 * UNITS):
                first(last, u, u < UNITS)
                third(last - (u < 2), (u - 2) % (2 * UNITS))
                second(last - (u < 1), (u - 1) % (2 * UNITS))
            second(last, 2 * UNITS - 1)
            third(last, 2 * UNITS - 2)
            third(last, 2 * UNITS - 1)
            for hf in range(2):
                dve.wait_ge(sum_done[0], hf + 1)
                nc.vector.tensor_copy(res[:, 0, hf * HALF:(hf + 1) * HALF], acc(0, hf)).then_inc(res_dve, 1)

        @block.tensor
        def _(pe):
            mm = nc.tensor.matmul

            def warm_up():
                pe.wait_ge(zeros, 1)
                for _ in range(WARM):
                    mm(bank[0][:, 0:E], ex[:, 0, 0:P], ex[:, 0, :], start=True, stop=True)

            def keep_warm(n):
                for _ in range(n):
                    mm(bank[0][0:PADW, 0:E], kt[:, 0, 0:PADW], kt[:, 0, 0:E], start=True, stop=True)

            def dora_update():
                pe.wait_ge(in_dora, 16)
                for m in range(2):
                    for k in range(KC):
                        ins = mm(bank[6 + m][:, k * E:(k + 1) * E], dr[:, 2 * m, k * P:(k + 1) * P], dr[:, 2 * m + 1, :],
                                 start=(k == 0), stop=True, skip_group_check=True)
                    ins.then_inc(dora_mm, 1)

            def turn(dst, src, n_, done):
                for c in range(KC):
                    ins = nc.tensor.transpose(dst[:, c * n_:(c + 1) * n_], src[:, c * P:(c + 1) * P], ident[0:n_, 0:n_])
                ins.then_inc(done, 1)

            def embed(t, halves=(0, 1)):
                at, n_ = TILES[t]
                o = E_BANK[0:n_, 0:E]
                for half in halves:
                    if t == 0:
                        pe.wait_ge(in_first[half], 32)
                    elif half == 0:
                        pe.wait_ge(in_x[t], 16)
                        pe.wait_ge(hg_done, t)
                        if t >= 2:
                            pe.wait_ge(v_done, t - 1)
                    for k in range(half * KD // 2, (half + 1) * KD // 2):
                        mm(o, xt[:, KD * at + k * n_:KD * at + (k + 1) * n_], wt[:, k, :], start=(k == 0), stop=False)
                    if half == 1:
                        if t == 0:
                            pe.wait_ge(in_add, 32)
                        mm(o, addsel[:, at:at + n_], addr[:, :], start=False, stop=True).then_inc(emb, 1)

            def turn_attn(t):
                n_ = TILES[t][1]
                pe.wait_ge(x2_done, t + 1)
                if t == 0:
                    pe.wait_ge(in_small, 16 * 2)
                if t:
                    pe.wait_ge(x2t_done, t)
                if t >= ROUTE:
                    pe.wait_ge(thi_done, t - ROUTE + 1)
                turn(T_BANK, x2[0:n_, t % 2, :], n_, x2t_mm)

            def turn_ffn(t):
                n_ = TILES[t][1]
                pe.wait_ge(tn_done, t + 1)
                pe.wait_ge(x2t_done, min(t + ROUTE, NT))
                if t:
                    pe.wait_ge(thi_done, t)
                turn(T_BANK, tn[0:n_, t % 2, :], n_, tt_mm)

            def queries_keys(t, parts=(0, 1)):
                for i in parts:
                    w = (wqv[:, 0], pw[:, 2])[i]
                    if i == 0:
                        pe.wait_ge(x2t_done, t + 1)
                        if t:
                            pe.wait_ge(qk_done, t)
                        else:
                            pe.wait_ge(dora_w, 2)
                            pe.wait_ge(in_ko, 32)
                    for c in range(KC):
                        o = (i * KC + c) * P
                        for k in range(KC):
                            ins = mm(Q_BANK[:, o:o + P], w[:, k, c * P:(c + 1) * P], x2t[:, t % 2, k, :],
                                     start=(k == 0), stop=(k == KC - 1))
                    if i == 1:
                        ins.then_inc(qk_mm, 1)

            def values_mm(t):
                n_ = TILES[t][1]
                pe.wait_ge(hg_done, min(t + 2, NT))
                for k in range(KC):
                    ins = mm(E_BANK[0:n_, 0:E], x2t[:, t % 2, k, 0:n_], wqv[:, 1, k, :], start=(k == 0), stop=(k == KC - 1))
                ins.then_inc(v_mm, 1)

            def scores(t, i):
                c, j0, nj = groups(t)[i]
                k = group_at[t] + i
                pe.wait_ge(qbd_pool if c else qbd_dve, t + 1)
                pe.wait_ge(qk_done, t + 1)
                if k == 0:
                    pe.wait_ge(set_up, 4)
                if k >= 2:
                    pe.wait_ge(s_sub, k - 1)
                if t == NT - 1 and i < 2:
                    pe.wait_ge((xg_done, li_done)[k % 2], 1)
                for j in range(nj):
                    pos = t * PPT + j0 + j
                    ins = mm(bank[k % 2][:, j * P:(j + 1) * P], qbd[:, c, pos, :, :].rearrange("p h q -> p (h q)"),
                             kt[:, c, pos * IMGS:pos * IMGS + P], start=True, stop=True)
                ins.then_inc(s_mm, 1)

            def turn_p(t):
                n_ = TILES[t][1]
                pe.wait_ge(p_done, t + 1)
                if t:
                    pe.wait_ge(h2_done, t)
                if t >= TURN - ATTN:
                    pe.wait_ge(rt_done, t - (TURN - ATTN) + 1)
                for c, o in enumerate((P_BANK, A_BANK)):
                    ins = nc.tensor.transpose(o[0:n_, 0:P], pr[:, t % 2, c * n_:(c + 1) * n_], ident)
                ins.then_inc(pt_mm, 1)

            def mix(t):
                n_ = TILES[t][1]
                pe.wait_ge(v_done, t + 1)
                if t:
                    pe.wait_ge(ot_done, t)
                for c, spread in enumerate((pt_act, pt_dve)):
                    pe.wait_ge(spread, t + 1)
                    for h in range(HPC):
                        ins = mm(O_BANK[:, c * P:(c + 1) * P], vbd[0:n_, c, h * P:(h + 1) * P],
                                 ptb[0:n_, c * HPC + h, :, :].rearrange("p n q -> p (n q)"),
                                 start=(h == 0), stop=(h == HPC - 1))
                ins.then_inc(o_mm, 1)

            def project(t):
                n_ = TILES[t][1]
                pe.wait_ge(ot_done, t + 1)
                for k in range(KC):
                    ins = mm(projection(t), ot[:, t % 2, k, 0:n_], pw[:, 3, k, :], start=(k == 0), stop=(k == KC - 1))
                ins.then_inc(a_mm, 1)

            def gate_mm(t):
                at, n_ = TILES[t]
                pe.wait_ge(tt_done, t + 1)
                pe.wait_ge(pt_act, min(t + ROUTE - ATTN + 1, NT))
                if t:
                    pe.wait_ge(rt_done, t)
                else:
                    pe.wait_ge(in_gate, 32)
                o = P_BANK[0:n_, 0:EXPERTS]
                for k in range(KC):
                    mm(o, tt[:, k, at:at + n_], gw[:, k, :], start=(k == 0), stop=False)
                mm(o, ones[0:1, 0:n_], gb[:, :], start=False, stop=True).then_inc(g_mm, 1)

            def turn_route(t):
                n_ = TILES[t][1]
                pe.wait_ge(r_done, t + 1)
                nc.tensor.transpose(P_BANK[0:EXPERTS, 0:n_], route[0:n_, t, :], ident[0:n_, 0:n_]).then_inc(rt_mm, 1)

            def exact(o, w, x, first, last):
                (w_hi_, w_lo_), (x_hi_, x_lo_) = w, x
                mm(o, w_hi_, x_hi_, start=first, stop=False)
                mm(o, w_hi_, x_lo_, start=False, stop=False)
                return mm(o, w_lo_, x_hi_, start=False, stop=last)

            def up(at, u):
                s, j, hf = u // UNITS, u % 2, (u % UNITS) // 2
                cols = slice(hf * HALF, (hf + 1) * HALF)
                if isinstance(at, int) and at == 0 and u == 0:
                    pe.wait_ge(tlo_done, EARLY)
                if u % UNITS == 0:
                    pe.wait_ge(w_lo, at * (2 * UNITS) + u + UNITS - 1)
                if not isinstance(at, int) or at * 2 * UNITS + u >= 2:
                    pe.wait_ge(xg_done, at * (2 * UNITS) + u - 1)
                    pe.wait_ge(li_done, at * (2 * UNITS) + u - 1)
                for m in range(2):
                    for k in range(KC):
                        ins = exact(bank[2 * (u % 2) + m][:, 0:HALF],
                                    (w1(whi, s)[:, k, 2 * m + j, :], w1(wlo, s)[:, k, 2 * m + j, :]),
                                    (thi[:, k, cols], tlo[:, k, cols]), k == 0, k == KC - 1)
                ins.then_inc(up_mm, 1)

            def down(at, u, last=False):
                s, j, hf, b = u // UNITS, u % 2, (u % UNITS) // 2, u % RING
                if u % UNITS == 0:
                    pe.wait_ge(w_lo, at * (2 * UNITS) + u + UNITS)
                pe.wait_ge(lo_done, at * (2 * UNITS) + u + 1)
                for c in range(KC):
                    ins = exact(acc(c, hf), (w2(whi, s)[:, j, c, :], w2(wlo, s)[:, j, c, :]),
                                (shi[:, b, :], slo[:, b, :]), False, last)
                    if last:
                        ins.then_inc(sum_done[c], 1)

            def start_sum(c, hf):
                lo, hi = hf * HALF, (hf + 1) * HALF
                pe.wait_ge(rt_done, (EARLY, NT)[hf])
                pe.wait_ge(hx_done, (EARLY, NT)[hf])
                mm(acc(c, hf), b2s[:, c * P:(c + 1) * P], rt[:, lo:hi], start=True, stop=False)
                for t, (at, n_) in enumerate(TILES):
                    a, b = max(at, lo), min(at + n_, hi)
                    if a < b:
                        mm(acc(c, hf)[:, a - lo:b - lo], hx[0:n_, t, c * P:(c + 1) * P], ident[0:n_, a - at:b - at],
                           start=False, stop=False)

            warm_up()
            embed(0)
            dora_update()
            embed(1)
            turn_attn(0)
            pe.wait_ge(dora_sq, 2)
            mm(A_BANK[:, 0:2], ones, ss[:, :], start=True, stop=True).then_inc(dora_sum, 1)
            queries_keys(0)
            values_mm(0)
            embed(2, (0,))
            scores(0, 0)
            for step in range(ATTN, NT + ATTN):
                fresh, qkv, attn, route_t, turned = in_flight(step)
                if turned is not None:
                    turn_route(turned)
                scores(attn, 1)
                if attn == NT - 1:
                    pe.wait_ge(v_done, NT)
                    start_sum(0, 0)
                for i in range(2, len(groups(attn))):
                    scores(attn, i)
                if step == ATTN:
                    turn_attn(1)
                elif fresh is not None:
                    embed(fresh, (0,))
                elif qkv is not None:
                    queries_keys(qkv, (0,))
                if route_t is not None:
                    turn_ffn(route_t)
                if fresh is not None:
                    embed(fresh, (1,))
                elif qkv is not None:
                    queries_keys(qkv, (1,))
                else:
                    start_sum(1, 0)
                turn_p(attn)
                if fresh is not None:
                    queries_keys(qkv)
                if qkv is not None:
                    values_mm(qkv)
                if attn == NT - 2:
                    up(0, 0)
                if attn == NT - 1:
                    keep_warm(3)
                if route_t is not None:
                    gate_mm(route_t)
                mix(attn)
                if fresh is not None:
                    turn_attn(fresh)
                if qkv is not None:
                    scores(qkv, 0)
                else:
                    turn_route(route_t)
                project(attn)

            up(0, 1)
            down(0, 0)
            turn_ffn(NT - 1)
            keep_warm(1)
            gate_mm(NT - 1)
            keep_warm(1)
            pe.wait_ge(tlo_done, NT)
            up(0, 2)
            turn_route(NT - 1)
            up(0, 3)
            pe.wait_ge(rt_done, NT)
            mm(T_BANK[:, 0:HALF], ones[0:1, :], rt[0:1, HALF:TOK], start=True, stop=True).then_inc(rb_mm, 1)
            start_sum(1, 1)
            pe.wait_ge(rb_in[0][1], 16)
            start_sum(0, 1)
            for u in range(2 * UNITS):
                if u:
                    down(0, u)
                up((u + LAG) // (2 * UNITS), (u + LAG) % (2 * UNITS))
            with pe.Fori(1, EXPERTS // 2 - 1) as i:
                for u in range(2 * UNITS):
                    down(i, u)
                    if u + LAG < 2 * UNITS:
                        up(i, u + LAG)
                    else:
                        up(i + 1, u + LAG - 2 * UNITS)
            for u in range(2 * UNITS):
                if u == 2 * UNITS - 2:
                    keep_warm(3)
                down(EXPERTS // 2 - 1, u, u in (2 * UNITS - 3, 2 * UNITS - 1))
                if u + LAG < 2 * UNITS:
                    up(EXPERTS // 2 - 1, u + LAG)


def kernel(**inputs):
    import numpy as np
    import concourse.bacc as bacc
    from concourse import mybir as mb
    from concourse.bass_utils import run_bass_kernel_spmd as run

    a = {k: np.asarray(v) for k, v in inputs.items()}
    f = np.float32
    x = a["x"].reshape(IMGS, CH, GRID, PATCH, GRID, PATCH).transpose(1, 3, 5, 2, 4, 0).reshape(D_IN, TOK - IMGS)
    x_t = np.concatenate([np.zeros((D_IN, IMGS), f), x], axis=1)
    add_rows = np.concatenate([a["L0_tok_pos_embedding"][0], a["L0_tok_b"][None], a["L0_tok_cls_token"][0]])
    sel = np.zeros((ADD_ROWS, TOK), f)
    for p in range(POS):
        sel[p, p * IMGS:(p + 1) * IMGS] = 1
    sel[POS, IMGS:] = 1
    sel[POS + 1, :IMGS] = 1

    def col(v):
        return v.reshape(KC, P).T

    w1 = a["L0_ffn_mlp1_w"].reshape(EXPERTS, INNER, 2, KC, P).transpose(0, 4, 3, 2, 1).reshape(EXPERTS, P, -1)
    w2 = a["L0_ffn_mlp2_w"].reshape(EXPERTS, E, KC, P).transpose(0, 3, 2, 1).reshape(EXPERTS, P, -1)
    b1 = a["L0_ffn_mlp1_b"].reshape(EXPERTS, KC, P, 2).transpose(0, 2, 3, 1).reshape(EXPERTS, P, 4)
    consts = np.zeros((P, CONST_COLS), f)
    consts[:, :P] = np.eye(P)
    consts[:, P:MASK_AT] = 1
    consts[np.arange(P), MASK_AT + np.arange(P) // HD] = 1
    for i, name in enumerate(("L0_attn_bias_q", "L0_attn_k_b", "L0_ffn_scale")):
        consts[:, COL_AT + i * KC:COL_AT + (i + 1) * KC] = col(a[name])
    consts[:, MAG_AT:GATE_AT] = np.stack([a["L0_attn_mag_q"], a["L0_attn_mag_v"]]).reshape(1, 2)
    consts[:, GATE_AT:] = a["L0_ffn_gate_w"].T.reshape(KC, P, EXPERTS).transpose(1, 0, 2).reshape(P, -1)
    tiles = [x_t[:, at:at + n].reshape(KD, P, n).transpose(1, 0, 2).reshape(P, KD * n) for at, n in TILES]
    arrays = {
        "x_t": np.concatenate(tiles, axis=1), "w_tok": a["L0_tok_W"], "add_rows": add_rows, "add_sel": sel,
        "proj": np.stack([a["L0_attn_dir_q"].T, a["L0_attn_dir_v"].T, a["L0_attn_k_w"].T, a["L0_attn_out_w"].T]),
        "dora": np.stack([a["L0_attn_A_q"], a["L0_attn_B_q"].T, a["L0_attn_A_v"], a["L0_attn_B_v"].T], axis=1),
        "rows": np.stack([a["L0_tok_gamma"], a["L0_tok_beta"], a["L0_attn_bias_v"], a["L0_attn_out_b"]]),
        "gate_b": a["L0_ffn_gate_b"].reshape(1, EXPERTS), "b2": a["L0_ffn_mlp2_b"],
        "experts": np.concatenate([w1, w2, b1], axis=2), "consts": consts,
    }
    arrays = {k: np.ascontiguousarray(v) for k, v in arrays.items()}
    nc = bacc.Bacc("TRN2", target_bir_lowering=False, num_devices=1)
    args = [nc.dram_tensor(f"in_{k}", v.shape, mb.dt.from_np(v.dtype), kind="ExternalInput").ap()
            for k, v in arrays.items()]
    out = nc.dram_tensor("out", [E, TOK], mb.dt.float32, kind="ExternalOutput").ap()
    build(nc, *args, out)
    r = run(nc, [{f"in_{k}": v for k, v in arrays.items()}], core_ids=[0])
    return r.results[0]["out"].reshape(E, POS, IMGS).transpose(2, 1, 0).copy()
```
